# Optimizing a Trainium2 kernel written in Bass

```python
import numpy as np
import jax
import jax.numpy as jnp

def _softmax(x, axis=-1):
    return jax.nn.softmax(x, axis=axis)

def _gelu(x):
    return jax.nn.gelu(x, approximate=True)

def _silu(x):
    return jax.nn.silu(x)

def _sigmoid(x):
    return jax.nn.sigmoid(x)

def _layernorm(x, axis=-1, eps=1e-05):
    m = jnp.mean(x, axis=axis, keepdims=True)
    v = jnp.var(x, axis=axis, keepdims=True)
    return (x - m) / jnp.sqrt(v + eps)

def _scatter_add(tgt, idx, src, axis=0):
    return tgt.at[idx].add(src)

def _segment_sum(src, seg, n):
    return jax.ops.segment_sum(src, seg, n)
kernel_name = 'mk_gnn_ffn_d1_gnn_r32_f297f7'

def setup_inputs(seed: int=0):
    np.random.seed(seed)
    _w = jnp.asarray

    def _rec_inputs():
        import jax
        import jax.numpy as jnp
        _gk = jax.random.key(seed)
        x = -8.776e-05 + 1 * jax.random.normal(jax.random.fold_in(_gk, 1), (625, 256), jnp.float32)
        src = jax.random.randint(jax.random.fold_in(_gk, 2), (20000,), 0, 625, jnp.int32)
        dst = jnp.minimum((625 * jax.random.uniform(jax.random.fold_in(_gk, 3), (20000,)) ** 2.0).astype(jnp.int32), 19999)
        _o = jnp.argsort(dst, stable=True)
        src = src[_o]
        dst = dst[_o]
        edge_attr_256 = 2.93046e-05 + 1.00006 * jax.random.normal(jax.random.fold_in(_gk, 11), (20000, 256), jnp.float32)
        return (x, src, dst, edge_attr_256)
    x, src, dst, edge_attr_256 = _rec_inputs()

    def _L0_gnn_setup():
        import jax, jax.numpy as jnp
        import numpy as np
        N = 625
        E = 10000
        F = 256
        EPS = 1e-05

        def _bn(h, gamma, beta):
            mu = h.mean(axis=0)
            var = h.var(axis=0)
            return (h - mu) * jax.lax.rsqrt(var + EPS) * gamma + beta
        key = jax.random.key(seed)
        ks = jax.random.split(key, 8)
        s = 0.02
        inp = {'x': jax.random.normal(ks[0], (N, F), jnp.float32), 'edge_index': jax.random.randint(ks[1], (2, E), 0, N), 'edge_attr': jax.random.normal(ks[2], (E, F), jnp.float32), 'W1f': jax.random.normal(ks[3], (3 * F, F), jnp.float32) * s, 'b1f': jnp.zeros((F,), jnp.float32), 'W2f': jax.random.normal(ks[4], (F, F), jnp.float32) * s, 'b2f': jnp.zeros((F,), jnp.float32), 'W1m': jax.random.normal(ks[5], (3 * F, F), jnp.float32) * s, 'b1m': jnp.zeros((F,), jnp.float32), 'W2m': jax.random.normal(ks[6], (F, F), jnp.float32) * s, 'b2m': jnp.zeros((F,), jnp.float32), 'g_int': jnp.ones((F,), jnp.float32), 'beta_int': jnp.zeros((F,), jnp.float32), 'g_bn': jnp.ones((F,), jnp.float32), 'beta_bn': jnp.zeros((F,), jnp.float32)}
        return inp
    _L0_gnn_all = _L0_gnn_setup()
    _L0_gnn_in = {k: v for k, v in _L0_gnn_all.items() if k in ('W1f', 'b1f', 'W2f', 'b2f', 'W1m', 'b1m', 'W2m', 'b2m', 'g_int', 'beta_int', 'g_bn', 'beta_bn')}
    del _L0_gnn_all

    def _L0_ffn_setup():
        import jax, jax.numpy as jnp
        import numpy as np
        D_MODEL = 256
        EXPERT_DIM = 512
        NUM_EXPERTS = 8
        TOP_K = 2
        SEQ_LEN = 64
        BATCH = 2
        key = jax.random.key(seed)
        ks = jax.random.split(key, 8)
        s = 0.02
        x = jax.random.normal(ks[0], (SEQ_LEN, BATCH, D_MODEL), dtype=jnp.float32)
        Wg = jax.random.normal(ks[1], (D_MODEL, NUM_EXPERTS), dtype=jnp.float32) * s
        bg = jax.random.normal(ks[2], (NUM_EXPERTS,), dtype=jnp.float32) * s
        bias = jnp.zeros((NUM_EXPERTS,), dtype=jnp.float32)
        W1 = jax.random.normal(ks[3], (NUM_EXPERTS, D_MODEL, EXPERT_DIM), dtype=jnp.float32) * s
        b1 = jax.random.normal(ks[4], (NUM_EXPERTS, EXPERT_DIM), dtype=jnp.float32) * s
        W2 = jax.random.normal(ks[5], (NUM_EXPERTS, EXPERT_DIM, D_MODEL), dtype=jnp.float32) * s
        b2 = jax.random.normal(ks[6], (NUM_EXPERTS, D_MODEL), dtype=jnp.float32) * s
        return {'x': x, 'Wg': Wg, 'bg': bg, 'bias': bias, 'W1': W1, 'b1': b1, 'W2': W2, 'b2': b2}
    _L0_ffn_all = _L0_ffn_setup()
    _L0_ffn_in = {k: v for k, v in _L0_ffn_all.items() if k in ('Wg', 'bg', 'bias', 'W1', 'b1', 'W2', 'b2')}
    del _L0_ffn_all
    return {'x': x, 'src': src, 'dst': dst, 'edge_attr_256': edge_attr_256, 'L0_gnn_W1f': _L0_gnn_in['W1f'], 'L0_gnn_b1f': _L0_gnn_in['b1f'], 'L0_gnn_W2f': _L0_gnn_in['W2f'], 'L0_gnn_b2f': _L0_gnn_in['b2f'], 'L0_gnn_W1m': _L0_gnn_in['W1m'], 'L0_gnn_b1m': _L0_gnn_in['b1m'], 'L0_gnn_W2m': _L0_gnn_in['W2m'], 'L0_gnn_b2m': _L0_gnn_in['b2m'], 'L0_gnn_g_int': _L0_gnn_in['g_int'], 'L0_gnn_beta_int': _L0_gnn_in['beta_int'], 'L0_gnn_g_bn': _L0_gnn_in['g_bn'], 'L0_gnn_beta_bn': _L0_gnn_in['beta_bn'], 'L0_ffn_Wg': _L0_ffn_in['Wg'], 'L0_ffn_bg': _L0_ffn_in['bg'], 'L0_ffn_bias': _L0_ffn_in['bias'], 'L0_ffn_W1': _L0_ffn_in['W1'], 'L0_ffn_b1': _L0_ffn_in['b1'], 'L0_ffn_W2': _L0_ffn_in['W2'], 'L0_ffn_b2': _L0_ffn_in['b2']}

def reference(x, src, dst, edge_attr_256, L0_gnn_W1f, L0_gnn_b1f, L0_gnn_W2f, L0_gnn_b2f, L0_gnn_W1m, L0_gnn_b1m, L0_gnn_W2m, L0_gnn_b2m, L0_gnn_g_int, L0_gnn_beta_int, L0_gnn_g_bn, L0_gnn_beta_bn, L0_ffn_Wg, L0_ffn_bg, L0_ffn_bias, L0_ffn_W1, L0_ffn_b1, L0_ffn_W2, L0_ffn_b2):
    import jax
    import jax.numpy as jnp

    def _L0_gnn_ref(x, edge_index, edge_attr, W1f, b1f, W2f, b2f, W1m, b1m, W2m, b2m, g_int, beta_int, g_bn, beta_bn):
        import jax, jax.numpy as jnp
        import numpy as np
        N = 625
        E = 10000
        F = 256
        EPS = 1e-05

        def _bn(h, gamma, beta):
            mu = h.mean(axis=0)
            var = h.var(axis=0)
            return (h - mu) * jax.lax.rsqrt(var + EPS) * gamma + beta
        src = edge_index[0]
        dst = edge_index[1]
        h = jnp.concatenate([x[dst], x[src], edge_attr], axis=1)
        gate = jax.nn.sigmoid(_bn(jax.nn.silu(h @ W1f + b1f) @ W2f + b2f, g_int, beta_int))
        msg = gate * (jax.nn.silu(h @ W1m + b1m) @ W2m + b2m)
        agg = jax.ops.segment_sum(msg, dst, num_segments=N)
        return jax.nn.relu(x + _bn(agg, g_bn, beta_bn))

    def _L0_ffn_ref(x, Wg, bg, bias, W1, b1, W2, b2):
        import jax, jax.numpy as jnp
        import numpy as np
        D_MODEL = 256
        EXPERT_DIM = 512
        NUM_EXPERTS = 8
        TOP_K = 2
        SEQ_LEN = 64
        BATCH = 2
        x_flat = x.reshape(-1, D_MODEL)
        gate_logits = x_flat @ Wg + bg + bias
        topk_vals, topk_idx = jax.lax.top_k(gate_logits, TOP_K)
        topk_w = jax.nn.softmax(topk_vals, axis=-1)
        combine = (jax.nn.one_hot(topk_idx, NUM_EXPERTS, dtype=x.dtype) * topk_w[..., None]).sum(axis=1)
        h = jax.nn.relu(jnp.einsum('td,edh->teh', x_flat, W1) + b1)
        y = jnp.einsum('teh,ehd->ted', h, W2) + b2
        out = jnp.einsum('ted,te->td', y, combine)
        return out.reshape(x.shape)
    edge_index = jnp.stack([src, dst])
    x = x + _L0_gnn_ref(_layernorm(x, axis=-1), edge_index, edge_attr_256, L0_gnn_W1f, L0_gnn_b1f, L0_gnn_W2f, L0_gnn_b2f, L0_gnn_W1m, L0_gnn_b1m, L0_gnn_W2m, L0_gnn_b2m, L0_gnn_g_int, L0_gnn_beta_int, L0_gnn_g_bn, L0_gnn_beta_bn)
    x = x + _L0_ffn_ref(_layernorm(x, axis=-1)[None], L0_ffn_Wg, L0_ffn_bg, L0_ffn_bias, L0_ffn_W1, L0_ffn_b1, L0_ffn_W2, L0_ffn_b2)[0]
    return x

_drawn_inputs = setup_inputs


def setup_inputs(seed=0):
    import zlib

    import numpy as np

    out = dict(_drawn_inputs(seed))
    spreads = {'L0_gnn_b1f': (0.0, 0.8),
     'L0_gnn_b2f': (0.0, 2.0),
     'L0_gnn_b1m': (0.0, 0.1),
     'L0_gnn_b2m': (0.0, 0.1),
     'L0_gnn_g_int': (1.0, 0.6),
     'L0_gnn_beta_int': (0.0, 0.8),
     'L0_gnn_g_bn': (1.0, 0.2),
     'L0_gnn_beta_bn': (0.0, 0.1),
     'L0_ffn_bias': (0.0, 0.288)}
    factors = {'L0_ffn_bg': 6.391, 'L0_ffn_b1': 23.648, 'L0_ffn_b2': 6.786}
    for name, (base, spread) in spreads.items():
        noise = np.random.default_rng([zlib.crc32(name.encode()), seed]).standard_normal(out[name].shape)
        drawn = base * np.exp(spread * noise) if base else spread * noise
        out[name] = jnp.asarray(drawn.astype(out[name].dtype))
    for name, factor in factors.items():
        out[name] = (out[name] * factor).astype(out[name].dtype)
    return out
```

```python
from contextlib import ExitStack

import concourse.bass as bass
from concourse import mybir

F32 = mybir.dt.float32
F32R = mybir.dt.float32r
I32 = mybir.dt.int32
ALU = mybir.AluOpType
ACT = mybir.ActivationFunctionType
AX_X = mybir.AxisListType.X

P = 128


def gnn_moe(nc, x, src, dst, edge_attr, W1f, b1f, W2f, b2f, W1m, b1m, W2m, b2m,
            g_int, beta_int, g_bn, beta_bn, Wg, bg, bias, W1, b1, W2, b2, out):
    N, F = x.shape
    E = edge_attr.shape[0]
    NE, _, H = W1.shape
    TP = 125
    NT = N // TP
    T = 4
    G = T * TP
    NG = E // G
    NPAIR = NG // 2
    KF = F // P
    KH = H // P
    F2 = 2 * F
    C = F2 // P
    EPS = 1e-5
    assert N == NT * TP and E == NG * G and NG % 2 == 0 and F == KF * P and F2 <= 512
    NPAD = N + N % 2
    HALF = [(0, 314), (314, NPAD)]
    PASSES = ((0, 0), (0, 1), (1, 0))

    table_dst = nc.dram_tensor("table_dst", (N, F2), F32, kind="Internal").ap()
    table_src = nc.dram_tensor("table_src", (N, F2), F32, kind="Internal").ap()
    z_gate = nc.dram_tensor("z_gate", (F, E), F32, kind="Internal").ap()
    z_val = nc.dram_tensor("z_val", (F, E), F32, kind="Internal").ap()

    ea_v = edge_attr.rearrange("(g p i) f -> g p i f", p=TP, i=T)
    src_v = src.rearrange("(g p i) -> g p i", p=TP, i=T)
    dst_v = dst.rearrange("(g p i) -> g p i", p=TP, i=T)
    zg_v = z_gate.rearrange("(j p) (g e) -> g p j e", p=P, e=G)
    zv_v = z_val.rearrange("(j p) (g e) -> g p j e", p=P, e=G)
    x_v = x.rearrange("(t p) f -> p t f", p=TP)
    out_v = out.rearrange("(t p) f -> p t f", p=TP)

    def column(v):
        return v.rearrange("(k p) -> p k", p=P)

    def spread(v, n):
        return v.rearrange("(a f) -> a f", a=1).broadcast_to((TP, n))

    whole = ExitStack()
    with whole:
        def sb(stack, name, shape, dt=F32):
            return stack.enter_context(nc.sbuf_tensor(name, shape, dt))

        def ps(stack, name, shape, dt=F32):
            return stack.enter_context(nc.psum_tensor(name, shape, dt))

        def sems(stack, *names):
            return [stack.enter_context(nc.semaphore(n)) for n in names]

        x_sb = sb(whole, "x_sb", [TP, NT, F])
        xln = sb(whole, "xln", [TP, NT, F])
        ident = sb(whole, "ident", [P, P])
        ln_stats = sb(whole, "ln_stats", [TP, NT, 6])
        ln_mv = sb(whole, "ln_mv", [TP, NT, 2])
        ln_std = sb(whole, "ln_std", [TP, NT])
        gate_stats = sb(whole, "gate_stats", [P, KF, NG * 6])
        dst_stored, src_stored, b1T_ok = sems(whole, "dst_stored", "src_stored", "b1T_ok")

        with ExitStack() as s:
            w1ab = sb(s, "w1ab", [P, 2 * KF, F2])
            b1_bc = sb(s, "b1_bc", [TP, F2])
            xT = sb(s, "xT", [P, KF, N])
            t_dst = sb(s, "t_dst", [TP, NT, F2])
            t_src = sb(s, "t_src", [TP, NT, F2])
            pT = [ps(s, f"pT{b}", [P, 512])[:, 0:KF * TP].rearrange("p (k n) -> p k n", k=KF) for b in range(2)]
            pA = [ps(s, f"pA{b}", [TP, F2]) for b in range(2)]
            pB = [ps(s, f"pB{b}", [TP, F2]) for b in range(2)]
            (x_in, w_in, zeroed, ident_ok, dve_done, std_ok, xln_ok, xT_psum, xT_ok, dst_psum, src_psum, dst_ok,
             src_ok) = sems(s, "x_in", "w_in", "zeroed", "ident_ok", "dve_done", "std_ok", "xln_ok",
                                    "xT_psum", "xT_ok", "dst_psum", "src_psum", "dst_ok", "src_ok")
            with nc.Block() as block:

                @block.sync
                def _(sp):
                    sp.dma_start(x_sb[:], x_v).then_inc(x_in, 16)
                    for b, w in enumerate((W1f, W1m)):
                        sp.dma_start(w1ab[:, :, b * F:(b + 1) * F],
                                     w[0:2 * F, :].rearrange("(k p) n -> p k n", p=P)).then_inc(w_in, 16)
                    for b, v in enumerate((b1f, b1m)):
                        sp.dma_start(b1_bc[:, b * F:(b + 1) * F], spread(v, F)).then_inc(w_in, 16)
                    sp.wait_ge(dst_ok, NT)
                    sp.dma_start(table_dst.rearrange("(t p) n -> p t n", p=TP), t_dst[:]).then_inc(dst_stored, 16)
                    sp.wait_ge(src_ok, NT)
                    sp.dma_start(table_src.rearrange("(t p) n -> p t n", p=TP), t_src[:]).then_inc(src_stored, 16)

                @block.gpsimd
                def _(pool):
                    nc.gpsimd.memset(ident[:], 0.0).then_inc(zeroed, 1)
                    pool.wait_ge(zeroed, 1)
                    nc.gpsimd.affine_select(out=ident[:], in_=ident[:], compare_op=ALU.not_equal, fill=1.0,
                                            base=0, pattern=[[-1, P]], channel_multiplier=1).then_inc(ident_ok, 1)

                @block.vector
                def _(dve):
                    dve.wait_ge(x_in, 16)
                    for t in range(NT):
                        nc.vector.bn_stats(ln_stats[:, t, :], x_sb[:, t, :]).then_inc(dve_done, 1)
                    for t in range(NT):
                        dve.wait_ge(dve_done, t + 1)
                        nc.vector.bn_aggr(ln_mv[:, t, :], ln_stats[:, t, :]).then_inc(dve_done, 1)
                    dve.wait_ge(dve_done, 2 * NT)
                    nc.vector.tensor_scalar(ln_std[:], ln_mv[:, :, 1], EPS, None, ALU.add).then_inc(dve_done, 1)
                    dve.wait_ge(std_ok, 1)
                    nc.vector.reciprocal(ln_std[:], ln_std[:]).then_inc(dve_done, 1)
                    dve.wait_ge(dve_done, 2 * NT + 2)
                    for t in range(NT):
                        nc.vector.tensor_scalar(xln[:, t, :], x_sb[:, t, :], ln_mv[:, t, 0:1], ln_std[:, t:t + 1],
                                                ALU.subtract, ALU.mult).then_inc(xln_ok, 1)
                    dve.wait_ge(w_in, 64)
                    for t in range(NT):
                        dve.wait_ge(dst_psum, t + 1)
                        nc.vector.tensor_tensor(t_dst[:, t, :], pA[t % 2][:], b1_bc[:], ALU.add).then_inc(dst_ok, 1)

                @block.scalar
                def _(act):
                    act.wait_ge(dve_done, 2 * NT + 1)
                    nc.scalar.activation(ln_std[:], ln_std[:], ACT.Sqrt).then_inc(std_ok, 1)
                    for t in range(NT):
                        act.wait_ge(xT_psum, t + 1)
                        nc.scalar.copy(xT[:, :, t * TP:(t + 1) * TP], pT[t % 2]).then_inc(xT_ok, 1)
                        if t:
                            act.wait_ge(src_psum, t)
                            nc.scalar.copy(t_src[:, t - 1, :], pB[(t - 1) % 2][:]).then_inc(src_ok, 1)
                    act.wait_ge(src_psum, NT)
                    nc.scalar.copy(t_src[:, NT - 1, :], pB[(NT - 1) % 2][:]).then_inc(src_ok, 1)

                @block.tensor
                def _(pe):
                    pe.wait_ge(ident_ok, 1)
                    pe.wait_ge(w_in, 64)

                    def products(t):
                        pe.wait_ge(xT_ok, t + 1)
                        for p, k0, free, done in ((pA, 0, dst_ok, dst_psum), (pB, KF, src_ok, src_psum)):
                            if t >= 2:
                                pe.wait_ge(free, t - 1)
                            for k in range(KF):
                                last = nc.tensor.matmul(p[t % 2][:], xT[:, k, t * TP:(t + 1) * TP],
                                                        w1ab[:, k0 + k, :], start=k == 0, stop=k == KF - 1)
                            last.then_inc(done, 1)

                    for t in range(NT):
                        pe.wait_ge(xln_ok, t + 1)
                        if t >= 2:
                            pe.wait_ge(xT_ok, t - 1)
                        for k in range(KF):
                            last = nc.tensor.transpose(pT[t % 2][:, k, :], xln[:, t, k * P:(k + 1) * P],
                                                       ident[0:TP, 0:TP])
                        last.then_inc(xT_psum, 1)
                        if t:
                            products(t - 1)
                    products(NT - 1)

        with ExitStack() as s:
            w1raw = sb(s, "w1raw", [P, KF, F2])
            w2raw = sb(s, "w2raw", [P, C, F])
            w1_hl = [sb(s, f"w1_{n}", [P, KF, F2], F32R) for n in ("hi", "lo")]
            w2_hl = [sb(s, f"w2_{n}", [P, C, F], F32R) for n in ("hi", "lo")]
            ea = [sb(s, f"ea{b}", [TP, T, F]) for b in range(2)]
            idx = [sb(s, f"idx{b}", [TP, 2, T], I32) for b in range(2)]
            pre = [sb(s, f"pre{b}", [TP, T, F2]) for b in range(2)]
            eaT_hl = [sb(s, f"eaT_{n}", [P, KF, G], F32R) for n in ("hi", "lo")]
            h_full = [sb(s, f"h_full{b}", [P, G]) for b in range(2)]
            h_hl = [sb(s, f"h_{n}", [P, C, G], F32R) for n in ("hi", "lo")]
            zg_st = sb(s, "zg_st", [P, KF, G])
            zv_st = sb(s, "zv_st", [P, KF, G])
            p_eaT = [ps(s, f"p_eaT{b}", [P, 512]) for b in range(KF)]
            p_pre = [ps(s, f"p_pre{b}", [P, 512]) for b in range(2)]
            p_hT = [ps(s, f"p_hT{b}", [P, 512]) for b in range(2)]
            p_z = [ps(s, f"p_z{b}", [P, 512]) for b in range(KF)]
            (w_in2, w_hi, w_lo, eaT_psum, eaT_hi, eaT_lo, pre_psum, pre_ok, hT_psum, silu_ok, h_lo_ok, zg_psum,
             zv_psum, zg_copied, zg_stats, zv_copied, zg_stored, zv_stored, gather_free) = sems(
                s, "w_in2", "w_hi", "w_lo", "eaT_psum", "eaT_hi_s", "eaT_lo_s", "pre_psum", "pre_ok", "hT_psum",
                "silu_ok", "h_lo_ok", "zg_psum", "zv_psum", "zg_copied", "zg_stats", "zv_copied", "zg_stored",
                "zv_stored", "gather_free")
            ea_in = sems(s, "ea_in0", "ea_in1")
            idx_in = sems(s, "idx_in0", "idx_in1")
            got_dst = sems(s, "got_dst0", "got_dst1")
            got_both = sems(s, "got_both0", "got_both1")
            with nc.Block() as block:

                @block.sync
                def _(sp):
                    for b, w in enumerate((W1f, W1m)):
                        sp.dma_start(w1raw[:, :, b * F:(b + 1) * F],
                                     w[2 * F:3 * F, :].rearrange("(k p) n -> p k n", p=P)).then_inc(w_in2, 16)
                    for b, w in enumerate((W2f, W2m)):
                        sp.dma_start(w2raw[:, b * KF:(b + 1) * KF, :],
                                     w.rearrange("(k p) n -> p k n", p=P)).then_inc(w_in2, 16)

                    def load(g, b):
                        sp.dma_start(idx[b][:, 0, :], dst_v[g]).then_inc(idx_in[b], 16)
                        sp.dma_start(idx[b][:, 1, :], src_v[g]).then_inc(idx_in[b], 16)
                        sp.dma_start(ea[b][:], ea_v[g]).then_inc(ea_in[b], 16)

                    def step(i, b, first=False, last=False):
                        g = 2 * i + b
                        if not last:
                            sp.wait_ge(eaT_psum, KF * g + KF)
                            sp.wait_ge(got_both[b], 16 * T * i + 16 * T)
                            load(g + 2, b)
                        if not (first and b == 0):
                            sp.wait_ge(zv_copied, KF * g)
                            sp.dma_start(zv_v[g - 1], zv_st[:]).then_inc(zv_stored, 16)
                        sp.wait_ge(zg_copied, KF * g + KF)
                        sp.dma_start(zg_v[g], zg_st[:]).then_inc(zg_stored, 16)

                    load(0, 0)
                    load(1, 1)
                    for b in range(2):
                        step(0, b, first=True)
                    with sp.Fori(1, NPAIR - 1) as i:
                        for b in range(2):
                            step(i, b)
                    for b in range(2):
                        step(NPAIR - 1, b, last=True)
                    sp.wait_ge(zv_copied, KF * NG)
                    sp.dma_start(zv_v[NG - 1], zv_st[:]).then_inc(zv_stored, 16)
                    sp.wait_ge(zv_stored, 16 * NG)
                    sp.wait_ge(zg_stored, 16 * NG)

                @block.gpsimd
                def _(pool):
                    def gather(i, b, first=False):
                        g = 2 * i + b
                        pool.wait_ge(idx_in[b], 32 * i + 32)
                        if not first:
                            pool.wait_ge(hT_psum, C * g - C)
                        pool.sem_inc(gather_free, 1)
                        pool.wait_ge(dst_stored, 16)
                        for t in range(T):
                            pool.indirect_dma_start(pre[b][:, t, :], None, table_dst, bass.IndirectOffsetOnAxis(
                                ap=idx[b][:, 0, t:t + 1], axis=0)).then_inc(got_dst[b], 16)
                        pool.wait_ge(got_dst[b], 16 * T * i + 16 * T)
                        pool.sem_inc(gather_free, 1)
                        pool.wait_ge(src_stored, 16)
                        for t in range(T):
                            pool.indirect_dma_start(pre[b][:, t, :], None, table_src, bass.IndirectOffsetOnAxis(
                                ap=idx[b][:, 1, t:t + 1], axis=0), compute_op=ALU.add).then_inc(got_both[b], 16)

                    for b in range(2):
                        gather(0, b, first=True)
                    with pool.Fori(1, NPAIR) as i:
                        for b in range(2):
                            gather(i, b)

                @block.scalar
                def _(act):
                    act.wait_ge(w_in2, 64)
                    nc.scalar.copy(w1_hl[0][:], w1raw[:]).then_inc(w_hi, 1)
                    nc.scalar.copy(w2_hl[0][:], w2raw[:]).then_inc(w_hi, 1)

                    def ea_hi(g, first=False):
                        for k in range(KF):
                            act.wait_ge(eaT_psum, KF * g + k + 1)
                            if not first:
                                act.wait_ge(pre_psum, T * g)
                            nc.scalar.copy(eaT_hl[0][:, k, :], p_eaT[k][:, 0:G]).then_inc(eaT_hi, 1)

                    def silu(g, branch, first):
                        for c in range(branch * KF, branch * KF + KF):
                            act.wait_ge(hT_psum, C * g + c + 1)
                            if not (first and c < 2):
                                act.wait_ge(h_lo_ok, C * g + c - 1)
                            if not first:
                                act.wait_ge(zv_psum if branch else zg_psum, KF * g)
                            nc.scalar.activation(h_hl[0][:, c, :], p_hT[c % 2][:, 0:G], ACT.Silu)
                            nc.scalar.activation(h_full[c % 2][:], p_hT[c % 2][:, 0:G],
                                                 ACT.Silu).then_inc(silu_ok, 1)

                    def store_values(g, first=False):
                        for j in range(KF):
                            act.wait_ge(zv_psum, KF * g + j + 1)
                            if not first:
                                act.wait_ge(zv_stored, 16 * g)
                            nc.scalar.copy(zv_st[:, j, :], p_z[j][:, 0:G]).then_inc(zv_copied, 1)

                    def step(i, b, first=False, last=False):
                        g = 2 * i + b
                        first, second, last = first and b == 0, first and b == 1, last and b == 1
                        silu(g, 0, first)
                        if not last:
                            ea_hi(g + 1)
                        if not first:
                            store_values(g - 1, first=second)
                        silu(g, 1, first)
                        for j in range(KF):
                            act.wait_ge(zg_psum, KF * g + j + 1)
                            if not first:
                                act.wait_ge(zg_stored, 16 * g)
                                act.wait_ge(zg_stats, KF * g)
                            nc.scalar.copy(zg_st[:, j, :], p_z[j][:, 0:G]).then_inc(zg_copied, 1)

                    ea_hi(0, first=True)
                    for b in range(2):
                        step(0, b, first=True)
                    with act.Fori(1, NPAIR - 1) as i:
                        for b in range(2):
                            step(i, b)
                    for b in range(2):
                        step(NPAIR - 1, b, last=True)
                    store_values(NG - 1)

                @block.vector
                def _(dve):
                    dve.wait_ge(w_hi, 1)
                    nc.vector.tensor_tensor(w1_hl[1][:], w1raw[:], w1_hl[0][:], ALU.subtract).then_inc(w_lo, 1)
                    dve.wait_ge(w_hi, 2)
                    nc.vector.tensor_tensor(w2_hl[1][:], w2raw[:], w2_hl[0][:], ALU.subtract).then_inc(w_lo, 1)

                    def ea_lo(g):
                        for k in range(KF):
                            dve.wait_ge(eaT_hi, KF * g + k + 1)
                            nc.vector.tensor_tensor(eaT_hl[1][:, k, :], p_eaT[k][:, 0:G], eaT_hl[0][:, k, :],
                                                    ALU.subtract).then_inc(eaT_lo, 1)

                    def h_lo(g, branch):
                        for c in range(branch * KF, branch * KF + KF):
                            dve.wait_ge(silu_ok, C * g + c + 1)
                            nc.vector.tensor_tensor(h_hl[1][:, c, :], h_full[c % 2][:], h_hl[0][:, c, :],
                                                    ALU.subtract).then_inc(h_lo_ok, 1)

                    def step(i, b, last=False):
                        g = 2 * i + b
                        dve.wait_ge(got_both[b], 16 * T * i + 16 * T)
                        for t in range(T):
                            dve.wait_ge(pre_psum, T * g + t + 1)
                            nc.vector.tensor_tensor(pre[b][:, t, :], p_pre[t % 2][0:TP, :], pre[b][:, t, :],
                                                    ALU.add).then_inc(pre_ok, 1)
                        h_lo(g, 0)
                        if not (last and b == 1):
                            ea_lo(g + 1)
                        h_lo(g, 1)
                        for j in range(KF):
                            dve.wait_ge(zg_copied, KF * g + j + 1)
                            nc.vector.bn_stats(gate_stats[:, j, bass.ds(g * 6, 6)],
                                               zg_st[:, j, :]).then_inc(zg_stats, 1)

                    ea_lo(0)
                    with dve.Fori(0, NPAIR - 1) as i:
                        for b in range(2):
                            step(i, b)
                    for b in range(2):
                        step(NPAIR - 1, b, last=True)

                @block.tensor
                def _(pe):
                    def transpose_ea(g, i, b):
                        pe.wait_ge(ea_in[b], 16 * i + 16)
                        for k in range(KF):
                            for t in range(T):
                                last = nc.tensor.transpose(p_eaT[k][:, t * TP:(t + 1) * TP],
                                                           ea[b][:, t, k * P:(k + 1) * P], ident[0:TP, 0:TP])
                            last.then_inc(eaT_psum, 1)

                    def first_layer(g, first):
                        pe.wait_ge(eaT_hi, KF * g + KF)
                        pe.wait_ge(eaT_lo, KF * g + KF)
                        for t in range(T):
                            if not (first and t < 2):
                                pe.wait_ge(pre_ok, T * g + t - 1)
                            n = 0
                            for k in range(KF):
                                for wp, dp in PASSES:
                                    last = nc.tensor.matmul(p_pre[t % 2][0:TP, :],
                                                            eaT_hl[dp][:, k, t * TP:(t + 1) * TP],
                                                            w1_hl[wp][:, k, :], start=n == 0, stop=n == 5)
                                    n += 1
                            last.then_inc(pre_psum, 1)

                    def transpose_pre(g, b, branch, first):
                        pe.wait_ge(pre_ok, T * g + T)
                        for c in range(branch * KF, branch * KF + KF):
                            if not (first and c < 2):
                                pe.wait_ge(silu_ok, C * g + c - 1)
                            for t in range(T):
                                last = nc.tensor.transpose(p_hT[c % 2][:, t * TP:(t + 1) * TP],
                                                           pre[b][:, t, c * P:(c + 1) * P], ident[0:TP, 0:TP])
                            last.then_inc(hT_psum, 1)

                    def second_layer(g, branch, first=False):
                        pe.wait_ge(h_lo_ok, C * g + branch * KF + KF)
                        for j in range(KF):
                            if branch:
                                pe.wait_ge(zg_copied, KF * g + j + 1)
                            elif not first:
                                pe.wait_ge(zv_copied, KF * g - KF + j + 1)
                            n = 0
                            for k in range(KF):
                                for wp, dp in PASSES:
                                    c = branch * KF + k
                                    last = nc.tensor.matmul(p_z[j][:, 0:G], w2_hl[wp][:, c, j * P:(j + 1) * P],
                                                            h_hl[dp][:, c, :], start=n == 0, stop=n == 5)
                                    n += 1
                            last.then_inc(zv_psum if branch else zg_psum, 1)

                    def step(i, b, first=False, last=False):
                        g = 2 * i + b
                        first, last = first and b == 0, last and b == 1
                        first_layer(g, first)
                        if not last:
                            transpose_ea(g + 1, i + b, 1 - b)
                        transpose_pre(g, b, 0, first)
                        if not first:
                            second_layer(g - 1, 1)
                        transpose_pre(g, b, 1, first)
                        second_layer(g, 0, first)

                    transpose_ea(0, 0, 0)
                    pe.wait_ge(w_lo, 2)
                    for b in range(2):
                        step(0, b, first=True)
                    with pe.Fori(1, NPAIR - 1) as i:
                        for b in range(2):
                            step(i, b)
                    for b in range(2):
                        step(NPAIR - 1, b, last=True)
                    second_layer(NG - 1, 1)

        agg = sb(whole, "agg", [TP, NT, F])
        with ExitStack() as s:
            vecs = sb(s, "vecs", [P, 4, KF])
            mv = sb(s, "mv", [P, KF, 2])
            tmp = sb(s, "tmp", [P, 4, KF])
            gate = [sb(s, f"gate{b}", [P, KF, G]) for b in range(2)]
            val = [sb(s, f"val{b}", [P, KF, G]) for b in range(2)]
            didx = [sb(s, f"didx{b}", [TP, T], I32) for b in range(2)]
            dstf = [sb(s, f"dstf{b}", [TP, T]) for b in range(2)]
            msgT = [sb(s, f"msgT{b}", [P, KF, G]) for b in range(2)]
            msg = [sb(s, f"msg{b}", [TP, T, 2, F], F32R) for b in range(2)]
            onehot = [sb(s, f"onehot{b}", [TP, T, N], F32R) for b in range(2)]
            node_id = sb(s, "node_id", [TP, N])
            zeros = sb(s, "zeros", [TP, F2])
            zeros_r = sb(s, "zeros_r", [TP, F2], F32R)
            p_msg = [ps(s, f"p_msg{h}", [P, 2, F]) for h in range(T // 2)]
            p_agg = [ps(s, f"p_agg{n}", [TP, 2, F]) for n in range(NT)]
            (v_in, ids_ok, chain, std2_ok, bn_ok, zero_ok, gate_ok, msgT_ok, msg_psum, msg_hi, msg_lo, dst_f,
             onehot_ok, summed, agg_hi_ok, agg_ok) = sems(
                s, "v_in", "ids_ok", "chain", "std2_ok", "bn_ok", "zero_ok", "gate_ok", "msgT_ok", "msg_psum",
                "msg_hi", "msg_lo", "dst_f", "onehot_ok", "summed", "agg_hi_ok", "agg_ok")
            z_in = sems(s, "z_in0", "z_in1")
            with nc.Block() as block:

                @block.sync
                def _(sp):
                    for n, v in enumerate((g_int, beta_int, b2f, b2m)):
                        sp.dma_start(vecs[:, n, :], column(v), allow_slow_non_contiguous=True).then_inc(v_in, 16)

                    def load(i, b, first=False):
                        g = 2 * i + b
                        if not first:
                            sp.wait_ge(dst_f, g - 1)
                        sp.dma_start(didx[b][:], dst_v[g]).then_inc(z_in[b], 16)
                        if not first:
                            sp.wait_ge(msgT_ok, KF * g - KF)
                        sp.dma_start(gate[b][:], zg_v[g]).then_inc(z_in[b], 16)
                        sp.dma_start(val[b][:], zv_v[g]).then_inc(z_in[b], 16)

                    for b in range(2):
                        load(0, b, first=True)
                    with sp.Fori(1, NPAIR) as i:
                        for b in range(2):
                            load(i, b)

                @block.gpsimd
                def _(pool):
                    nc.gpsimd.iota(node_id[:], pattern=[[1, N]], base=0, channel_multiplier=0,
                                   allow_small_or_imprecise_dtypes=True).then_inc(ids_ok, 1)

                @block.scalar
                def _(act):
                    act.wait_ge(chain, 2)
                    nc.scalar.activation(tmp[:, 0, :], tmp[:, 0, :], ACT.Sqrt).then_inc(std2_ok, 1)
                    act.wait_ge(bn_ok, 1)

                    def sigmoid(i, b):
                        act.wait_ge(z_in[b], 48 * i + 48)
                        for j in range(KF):
                            nc.scalar.activation(gate[b][:, j, :], gate[b][:, j, :], ACT.Sigmoid,
                                                 bias=tmp[:, 3, j:j + 1],
                                                 scale=tmp[:, 1, j:j + 1]).then_inc(gate_ok, 1)

                    def hi(g, b, first):
                        for h in range(T // 2):
                            act.wait_ge(msg_psum, 2 * g + h + 1)
                            if not first:
                                act.wait_ge(summed, g - 1)
                            nc.scalar.copy(msg[b][:, 2 * h:2 * h + 2, 0, :], p_msg[h][0:TP]).then_inc(msg_hi, 1)

                    def step(i, b, first=False, last=False):
                        if not (last and b == 1):
                            sigmoid(i + b, 1 - b)
                        hi(2 * i + b, b, first)

                    sigmoid(0, 0)
                    for b in range(2):
                        step(0, b, first=True)
                    with act.Fori(1, NPAIR - 1) as i:
                        for b in range(2):
                            step(i, b)
                    for b in range(2):
                        step(NPAIR - 1, b, last=True)
                    for n in range(NT):
                        act.wait_ge(summed, NG + 1)
                        nc.scalar.copy(agg[:, n, :], p_agg[n][:, 0, :]).then_inc(agg_hi_ok, 1)

                @block.vector
                def _(dve):
                    nc.vector.memset(zeros[:], 0.0).then_inc(zero_ok, 1)
                    dve.wait_ge(zero_ok, 1)
                    nc.vector.tensor_copy(zeros_r[:], zeros[:]).then_inc(zero_ok, 1)
                    for j in range(KF):
                        last = nc.vector.bn_aggr(mv[:, j, :], gate_stats[:, j, :])
                    last.then_inc(chain, 1)
                    dve.wait_ge(chain, 1)
                    nc.vector.tensor_scalar(tmp[:, 0, :], mv[:, :, 1], EPS, None, ALU.add).then_inc(chain, 1)
                    dve.wait_ge(std2_ok, 1)
                    nc.vector.reciprocal(tmp[:, 1, :], tmp[:, 0, :]).then_inc(chain, 1)
                    dve.wait_ge(chain, 3)
                    dve.wait_ge(v_in, 64)
                    nc.vector.tensor_tensor(tmp[:, 1, :], tmp[:, 1, :], vecs[:, 0, :], ALU.mult).then_inc(chain, 1)
                    nc.vector.tensor_tensor(tmp[:, 2, :], mv[:, :, 0], vecs[:, 2, :], ALU.add).then_inc(chain, 1)
                    dve.wait_ge(chain, 5)
                    nc.vector.tensor_tensor(tmp[:, 2, :], vecs[:, 2, :], tmp[:, 2, :],
                                            ALU.subtract).then_inc(chain, 1)
                    dve.wait_ge(chain, 6)
                    nc.vector.tensor_tensor(tmp[:, 3, :], tmp[:, 2, :], tmp[:, 1, :], ALU.mult).then_inc(chain, 1)
                    dve.wait_ge(chain, 7)
                    nc.vector.tensor_tensor(tmp[:, 3, :], tmp[:, 3, :], vecs[:, 1, :], ALU.add).then_inc(bn_ok, 1)

                    def message(g, b):
                        for j in range(KF):
                            dve.wait_ge(gate_ok, KF * g + j + 1)
                            nc.vector.scalar_tensor_tensor(out=msgT[b][:, j, :], in0=val[b][:, j, :],
                                                           scalar=vecs[:, 3, j:j + 1], in1=gate[b][:, j, :],
                                                           op0=ALU.add, op1=ALU.mult).then_inc(msgT_ok, 1)

                    def step(i, b, first=False, last=False):
                        g = 2 * i + b
                        if not (last and b == 1):
                            if not (first and b == 0):
                                dve.wait_ge(msg_psum, 2 * g)
                            message(g + 1, 1 - b)
                        if not first:
                            dve.wait_ge(summed, g - 1)
                        nc.vector.tensor_copy(dstf[b][:], didx[b][:]).then_inc(dst_f, 1)
                        dve.wait_ge(dst_f, g + 1)
                        for t in range(T):
                            nc.vector.tensor_scalar(onehot[b][:, t, :], node_id[:], dstf[b][:, t:t + 1], None,
                                                    ALU.is_equal).then_inc(onehot_ok, 1)
                        for h in range(T // 2):
                            dve.wait_ge(msg_hi, 2 * g + h + 1)
                            nc.vector.tensor_tensor(msg[b][:, 2 * h:2 * h + 2, 1, :], p_msg[h][0:TP],
                                                    msg[b][:, 2 * h:2 * h + 2, 0, :],
                                                    ALU.subtract).then_inc(msg_lo, 1)

                    dve.wait_ge(ids_ok, 1)
                    message(0, 0)
                    for b in range(2):
                        step(0, b, first=True)
                    with dve.Fori(1, NPAIR - 1) as i:
                        for b in range(2):
                            step(i, b)
                    for b in range(2):
                        step(NPAIR - 1, b, last=True)
                    for n in range(NT):
                        dve.wait_ge(agg_hi_ok, n + 1)
                        nc.vector.tensor_tensor(agg[:, n, :], p_agg[n][:, 1, :], agg[:, n, :],
                                                ALU.add).then_inc(agg_ok, 1)

                @block.tensor
                def _(pe):
                    def transpose_msg(g, b, first=False):
                        pe.wait_ge(msgT_ok, KF * g + KF)
                        for h in range(T // 2):
                            if not first:
                                pe.wait_ge(msg_lo, 2 * g - 1 + h)
                            for t in (2 * h, 2 * h + 1):
                                for j in range(KF):
                                    last = nc.tensor.transpose(p_msg[h][0:TP, t % 2, j * P:(j + 1) * P],
                                                               msgT[b][:, j, t * TP:(t + 1) * TP], ident[:])
                            last.then_inc(msg_psum, 1)

                    def scatter(g, b):
                        pe.wait_ge(onehot_ok, T * g + T)
                        pe.wait_ge(msg_lo, 2 * g + 2)
                        for t in range(T):
                            for n in range(NT):
                                last = nc.tensor.matmul(p_agg[n][:], onehot[b][:, t, n * TP:(n + 1) * TP],
                                                        msg[b][:, t, :, :], start=False, stop=False)
                        last.then_inc(summed, 1)

                    pe.wait_ge(zero_ok, 2)
                    for n in range(NT):
                        nc.tensor.matmul(p_agg[n][:], zeros_r[:, 0:TP], zeros_r[:], start=True, stop=False)
                    transpose_msg(0, 0, first=True)
                    transpose_msg(1, 1)
                    scatter(0, 0)
                    with pe.Fori(1, NPAIR) as i:
                        transpose_msg(2 * i, 0)
                        scatter(2 * i - 1, 1)
                        transpose_msg(2 * i + 1, 1)
                        scatter(2 * i, 0)
                    scatter(NG - 1, 1)
                    for n in range(NT):
                        last = nc.tensor.matmul(p_agg[n][:], zeros_r[:, 0:TP], zeros_r[:], start=False, stop=True)
                    last.then_inc(summed, 1)

        acc = sb(whole, "acc", [TP, NT, F])
        weight = sb(whole, "weight", [TP, NT, NE])
        xnT = sb(whole, "xnT", [P, KF, NPAD])
        xnT_hl = [sb(whole, f"xnT_{n}", [P, KF, NPAD], F32R) for n in ("hi", "lo")]
        b1T = sb(whole, "b1T", [P, NE * KH])
        with ExitStack() as s:
            ones = sb(s, "ones", [TP, TP])
            bn_rows = sb(s, "bn_rows", [TP, 2, F])
            gate_b = sb(s, "gate_b", [TP, 2, NE])
            dev = sb(s, "dev", [TP, NT, F])
            sq = sb(s, "sq", [TP, NT, F])
            rs = sb(s, "rs", [TP, F])
            wg_sb = sb(s, "wg_sb", [P, KF, NE])
            b1_sb = sb(s, "b1_sb", [NE * KH, P])
            b2_sb = sb(s, "b2_sb", [NE, F])
            expert_id = sb(s, "expert_id", [TP, NT, NE])
            rt = sb(s, "rt", [TP, 8, NT, NE])
            rs1 = sb(s, "rs1", [TP, 8, NT])
            wT = sb(s, "wT", [NE, NT, TP])
            p_sum = ps(s, "p_sum", [TP, 512])[:, 0:F]
            p_var = ps(s, "p_var", [TP, 512])[:, 0:F]
            p_xnT = [ps(s, f"p_xnT{b}", [P, 512])[:, 0:KF * TP].rearrange("p (k n) -> p k n", k=KF)
                     for b in range(2)]
            p_log = ps(s, "p_log", [TP, 512])[:, 0:NT * NE].rearrange("p (t e) -> p t e", t=NT)
            p_b1 = ps(s, "p_b1", [P, 512])
            p_b2 = [ps(s, f"p_b2_{b}", [TP, 512])[:, 0:F] for b in range(2)]
            (n_in, ids2_ok, ones_ok, chain2, sum_psum, sq_ok, var_psum, std3_ok, std4_ok, xn_ok, xnT_psum,
             xnT_copied, xnT_split, log_psum, exp_in, exp_ok, weight_ok, wT_psum, wT_ok, b1_psum, b2_psum,
             acc_ok, pad_ok) = sems(
                s, "n_in", "ids2_ok", "ones_ok", "chain2", "sum_psum", "sq_ok", "var_psum", "std3_ok", "std4_ok",
                "xn_ok", "xnT_psum", "xnT_copied", "xnT_split", "log_psum", "exp_in", "exp_ok", "weight_ok",
                "wT_psum", "wT_ok", "b1_psum", "b2_psum", "acc_ok", "pad_ok")
            with nc.Block() as block:

                @block.sync
                def _(sp):
                    for n, v in enumerate((g_bn, beta_bn)):
                        sp.dma_start(bn_rows[:, n, :], spread(v, F)).then_inc(n_in, 16)
                    for n, v in enumerate((bg, bias)):
                        sp.dma_start(gate_b[:, n, :], spread(v, NE)).then_inc(n_in, 16)
                    sp.dma_start(wg_sb[:], Wg.rearrange("(k p) e -> p k e", p=P)).then_inc(n_in, 16)
                    sp.dma_start(b1_sb[:], b1.rearrange("e (m p) -> (e m) p", p=P)).then_inc(n_in, 16)
                    sp.dma_start(b2_sb[:], b2).then_inc(n_in, 16)

                @block.gpsimd
                def _(pool):
                    nc.gpsimd.iota(expert_id[:], pattern=[[0, NT], [1, NE]], base=0, channel_multiplier=0,
                                   allow_small_or_imprecise_dtypes=True).then_inc(ids2_ok, 1)

                @block.scalar
                def _(act):
                    for t in range(NT):
                        act.wait_ge(chain2, t + 1)
                        nc.scalar.activation(sq[:, t, :], dev[:, t, :], ACT.Square).then_inc(sq_ok, 1)
                    act.wait_ge(chain2, NT + 1)
                    nc.scalar.activation(rs[:], rs[:], ACT.Sqrt).then_inc(std3_ok, 1)
                    act.wait_ge(std4_ok, 1)
                    nc.scalar.activation(ln_std[:], ln_std[:], ACT.Sqrt).then_inc(std4_ok, 1)
                    for t in range(NT):
                        act.wait_ge(xnT_psum, t + 1)
                        nc.scalar.copy(xnT[:, :, t * TP:(t + 1) * TP], p_xnT[t % 2]).then_inc(xnT_copied, 1)
                    act.wait_ge(xnT_copied, NT)
                    act.wait_ge(pad_ok, 1)
                    nc.scalar.copy(xnT_hl[0][:], xnT[:]).then_inc(xnT_split, 1)
                    act.wait_ge(exp_in, 1)
                    nc.scalar.activation(rs1[:, 3, :], rs1[:, 2, :], ACT.Exp).then_inc(exp_ok, 1)

                @block.vector
                def _(dve):
                    done = [0]

                    def then(ins):
                        done[0] += 1
                        ins.then_inc(chain2, 1)
                        dve.wait_ge(chain2, done[0])

                    def over_tiles(row):
                        return row.rearrange("p (a f) -> p a f", a=1).broadcast_to((TP, NT, F))

                    nc.vector.memset(ones[:], 1.0).then_inc(ones_ok, 1)
                    nc.vector.memset(xnT[:, :, N:NPAD], 0.0).then_inc(pad_ok, 1)
                    dve.wait_ge(sum_psum, 1)
                    for t in range(NT):
                        then(nc.vector.scalar_tensor_tensor(out=dev[:, t, :], in0=p_sum, scalar=-1.0 / N,
                                                            in1=agg[:, t, :], op0=ALU.mult, op1=ALU.add))
                    dve.wait_ge(var_psum, 1)
                    then(nc.vector.tensor_scalar(rs[:], p_var, 1.0 / N, EPS, ALU.mult, ALU.add))
                    dve.wait_ge(std3_ok, 1)
                    then(nc.vector.reciprocal(rs[:], rs[:]))
                    dve.wait_ge(n_in, 16 * 7)
                    then(nc.vector.tensor_tensor(rs[:], rs[:], bn_rows[:, 0, :], ALU.mult))
                    then(nc.vector.tensor_tensor(dev[:], dev[:], over_tiles(rs[:]), ALU.mult))
                    then(nc.vector.tensor_tensor(dev[:], dev[:], over_tiles(bn_rows[:, 1, :]), ALU.add))
                    then(nc.vector.tensor_tensor(dev[:], dev[:], xln[:], ALU.add))
                    then(nc.vector.scalar_tensor_tensor(out=x_sb[:], in0=dev[:], scalar=0.0, in1=x_sb[:],
                                                        op0=ALU.max, op1=ALU.add))
                    for t in range(NT):
                        last = nc.vector.bn_stats(ln_stats[:, t, :], x_sb[:, t, :])
                    then(last)
                    for t in range(NT):
                        last = nc.vector.bn_aggr(ln_mv[:, t, :], ln_stats[:, t, :])
                    then(last)
                    nc.vector.tensor_scalar(ln_std[:], ln_mv[:, :, 1], EPS, None, ALU.add).then_inc(std4_ok, 1)
                    dve.wait_ge(std4_ok, 2)
                    then(nc.vector.reciprocal(ln_std[:], ln_std[:]))
                    for t in range(NT):
                        nc.vector.tensor_scalar(xln[:, t, :], x_sb[:, t, :], ln_mv[:, t, 0:1], ln_std[:, t:t + 1],
                                                ALU.subtract, ALU.mult).then_inc(xn_ok, 1)
                    dve.wait_ge(b1_psum, 1)
                    nc.vector.tensor_copy(b1T[:], p_b1[:, 0:NE * KH]).then_inc(b1T_ok, 1)
                    dve.wait_ge(xnT_split, 1)
                    nc.vector.tensor_tensor(xnT_hl[1][:], xnT[:], xnT_hl[0][:], ALU.subtract).then_inc(xnT_split, 1)

                    logit, pick1, pick2, pen, rest = (rt[:, n] for n in range(5))
                    top1, top2, diff, expd, id1, id2, w1st, w2nd = (rs1[:, n, :] for n in range(8))

                    def over_experts(v):
                        return v.rearrange("p (t a) -> p t a", a=1).broadcast_to((TP, NT, NE))

                    def over_nodes(v):
                        return v.rearrange("p (a e) -> p a e", a=1).broadcast_to((TP, NT, NE))

                    def pick(table, top, ident_, chosen):
                        then(nc.vector.tensor_reduce(top, table, AX_X, ALU.max))
                        then(nc.vector.tensor_tensor(pen, table, over_experts(top), ALU.is_lt))
                        then(nc.vector.scalar_tensor_tensor(out=pen, in0=pen, scalar=float(NE), in1=expert_id[:],
                                                            op0=ALU.mult, op1=ALU.add))
                        then(nc.vector.tensor_reduce(ident_, pen, AX_X, ALU.min))
                        then(nc.vector.tensor_tensor(chosen, expert_id[:], over_experts(ident_), ALU.is_equal))

                    dve.wait_ge(log_psum, 1)
                    dve.wait_ge(ids2_ok, 1)
                    then(nc.vector.tensor_tensor(logit, p_log, over_nodes(gate_b[:, 0, :]), ALU.add))
                    then(nc.vector.tensor_tensor(logit, logit, over_nodes(gate_b[:, 1, :]), ALU.add))
                    pick(logit, top1, id1, pick1)
                    then(nc.vector.scalar_tensor_tensor(out=rest, in0=pick1, scalar=-3.0e38, in1=logit,
                                                        op0=ALU.mult, op1=ALU.add))
                    pick(rest, top2, id2, pick2)
                    nc.vector.tensor_tensor(diff, top2, top1, ALU.subtract).then_inc(exp_in, 1)
                    dve.wait_ge(exp_ok, 1)
                    then(nc.vector.tensor_scalar(w1st, expd, 1.0, None, ALU.add))
                    then(nc.vector.reciprocal(w1st, w1st))
                    then(nc.vector.tensor_tensor(w2nd, expd, w1st, ALU.mult))
                    then(nc.vector.tensor_tensor(pick1, pick1, over_experts(w1st), ALU.mult))
                    then(nc.vector.tensor_tensor(pick2, pick2, over_experts(w2nd), ALU.mult))
                    nc.vector.tensor_tensor(weight[:], pick1, pick2, ALU.add).then_inc(weight_ok, 1)
                    dve.wait_ge(wT_psum, 1)
                    nc.vector.tensor_copy(wT[:, 0:4, :], p_b1[0:NE, 0:4 * TP].rearrange(
                        "e (t n) -> e t n", t=4)).then_inc(wT_ok, 1)
                    nc.vector.tensor_copy(wT[:, 4, :], p_sum[0:NE, 0:TP]).then_inc(wT_ok, 1)
                    for t in range(NT):
                        dve.wait_ge(b2_psum, t + 1)
                        nc.vector.tensor_tensor(acc[:, t, :], p_b2[t % 2], x_sb[:, t, :],
                                                ALU.add).then_inc(acc_ok, 1)

                @block.tensor
                def _(pe):
                    pe.wait_ge(ones_ok, 1)
                    for t in range(NT):
                        last = nc.tensor.matmul(p_sum, ones[:], agg[:, t, :], start=t == 0, stop=t == NT - 1)
                    last.then_inc(sum_psum, 1)
                    pe.wait_ge(n_in, 16 * 7)
                    nc.tensor.transpose(p_b1[:, 0:NE * KH], b1_sb[:], ident[0:NE * KH, 0:NE * KH]).then_inc(
                        b1_psum, 1)
                    for t in range(NT):
                        pe.wait_ge(sq_ok, t + 1)
                        last = nc.tensor.matmul(p_var, ones[:], sq[:, t, :], start=t == 0, stop=t == NT - 1)
                    last.then_inc(var_psum, 1)
                    for t in range(NT):
                        pe.wait_ge(xn_ok, t + 1)
                        if t >= 2:
                            pe.wait_ge(xnT_copied, t - 1)
                        for k in range(KF):
                            last = nc.tensor.transpose(p_xnT[t % 2][:, k, :], xln[:, t, k * P:(k + 1) * P],
                                                       ident[0:TP, 0:TP])
                        last.then_inc(xnT_psum, 1)
                    pe.wait_ge(xnT_copied, NT)
                    for t in range(NT):
                        for k in range(KF):
                            last = nc.tensor.matmul(p_log[:, t, :], xnT[:, k, t * TP:(t + 1) * TP], wg_sb[:, k, :],
                                                    start=k == 0, stop=k == KF - 1)
                    last.then_inc(log_psum, 1)
                    pe.wait_ge(weight_ok, 1)
                    pe.wait_ge(b1T_ok, 1)
                    for t in range(NT):
                        to = p_b1[0:NE, t * TP:(t + 1) * TP] if t < 4 else p_sum[0:NE, 0:TP]
                        last = nc.tensor.transpose(to, weight[:, t, :], ident[0:TP, 0:TP])
                    last.then_inc(wT_psum, 1)
                    pe.wait_ge(wT_ok, 2)
                    for t in range(NT):
                        if t >= 2:
                            pe.wait_ge(acc_ok, t - 1)
                        nc.tensor.matmul(p_b2[t % 2], wT[:, t, :], b2_sb[:],
                                         start=True, stop=True).then_inc(b2_psum, 1)

        with ExitStack() as s:
            raw1 = [sb(s, f"raw1_{b}", [P, KF, H]) for b in range(2)]
            raw2 = [sb(s, f"raw2_{b}", [P, KH, F]) for b in range(2)]
            w1e = [[sb(s, f"w1e{b}_{n}", [P, KF, H], F32R) for n in ("hi", "lo")] for b in range(2)]
            w2e = [[sb(s, f"w2e{b}_{n}", [P, KH, F], F32R) for n in ("hi", "lo")] for b in range(2)]
            b1e = [sb(s, f"b1e{b}", [P, KH]) for b in range(2)]
            hid = [sb(s, f"hid{b}", [P, 314]) for b in range(2)]
            hT_hl = [[sb(s, f"hT{b}_{n}", [P, KH, NPAD], F32R) for n in ("hi", "lo")] for b in range(2)]
            p_h = [ps(s, f"p_h{b}", [P, 512]) for b in range(2)]
            p_y = [ps(s, f"p_y{b}", [P, 512]) for b in range(2)]
            (we_hi, we_lo, h_psum, hid_ok, h_split, y_psum, y_added, out_in, bias_ok) = sems(
                s, "we_hi", "we_lo", "h_psum", "hid_ok", "h_split", "y_psum", "y_added", "out_in", "bias_ok")
            raw_in = sems(s, "raw_in0", "raw_in1")
            NH = 2 * KH
            with nc.Block() as block:

                @block.sync
                def _(sp):
                    def load(i, b, first=False):
                        e = 2 * i + b
                        if not first:
                            sp.wait_ge(we_lo, 2 * e - 2)
                        sp.dma_start(raw1[b][:], W1[e].rearrange("(k p) n -> p k n", p=P)).then_inc(raw_in[b], 16)
                        sp.dma_start(raw2[b][:], W2[e].rearrange("(k p) n -> p k n", p=P)).then_inc(raw_in[b], 16)

                    for b in range(2):
                        load(0, b, first=True)
                    with sp.Fori(1, NE // 2) as i:
                        for b in range(2):
                            load(i, b)
                    sp.wait_ge(y_added, NT * NE)
                    sp.dma_start(out_v, acc[:]).then_inc(out_in, 16)
                    sp.wait_ge(out_in, 16)

                @block.scalar
                def _(act):
                    def split_hi(i, b, first=False):
                        act.wait_ge(raw_in[b], 32 * i + 32)
                        if not first:
                            act.wait_ge(h_psum, NH * (2 * i + b - 1))
                            act.wait_ge(y_psum, NT * (2 * i + b - 1))
                        nc.scalar.copy(w1e[b][0][:], raw1[b][:]).then_inc(we_hi, 1)
                        nc.scalar.copy(w2e[b][0][:], raw2[b][:]).then_inc(we_hi, 1)
                        nc.scalar.copy(b1e[b][:], b1T[:, bass.ds((2 * i + b) * KH, KH)]).then_inc(bias_ok, 1)

                    def hidden(i, b, first=False, start=False):
                        e = 2 * i + b
                        act.wait_ge(bias_ok, e + 1)
                        n = 0
                        for m in range(KH):
                            for lo, up in HALF:
                                act.wait_ge(h_psum, NH * e + n + 1)
                                if not (start and n < 2):
                                    act.wait_ge(h_split, NH * e + n - 1)
                                if not first:
                                    act.wait_ge(y_psum, NT * (e - 1))
                                nc.scalar.activation(hT_hl[b][0][:, m, lo:up], p_h[n % 2][:, 0:up - lo], ACT.Relu,
                                                     bias=b1e[b][:, m:m + 1])
                                nc.scalar.activation(hid[n % 2][:, 0:up - lo], p_h[n % 2][:, 0:up - lo], ACT.Relu,
                                                     bias=b1e[b][:, m:m + 1]).then_inc(hid_ok, 1)
                                n += 1

                    split_hi(0, 0, first=True)
                    split_hi(0, 1, first=True)
                    hidden(0, 0, first=True, start=True)
                    hidden(0, 1, first=True)
                    with act.Fori(1, NE // 2) as i:
                        split_hi(i, 0)
                        hidden(i, 0)
                        split_hi(i, 1)
                        hidden(i, 1)

                @block.vector
                def _(dve):
                    def split_lo(i, b):
                        e = 2 * i + b
                        dve.wait_ge(we_hi, 2 * e + 1)
                        nc.vector.tensor_tensor(w1e[b][1][:], raw1[b][:], w1e[b][0][:],
                                                ALU.subtract).then_inc(we_lo, 1)
                        dve.wait_ge(we_hi, 2 * e + 2)
                        nc.vector.tensor_tensor(w2e[b][1][:], raw2[b][:], w2e[b][0][:],
                                                ALU.subtract).then_inc(we_lo, 1)

                    def hidden_lo(i, b):
                        n = 0
                        for m in range(KH):
                            for lo, up in HALF:
                                dve.wait_ge(hid_ok, NH * (2 * i + b) + n + 1)
                                nc.vector.tensor_tensor(hT_hl[b][1][:, m, lo:up], hid[n % 2][:, 0:up - lo],
                                                        hT_hl[b][0][:, m, lo:up], ALU.subtract).then_inc(h_split, 1)
                                n += 1

                    def add(i, b, first=False):
                        e = 2 * i + b
                        for t in range(NT):
                            dve.wait_ge(y_psum, NT * e + t + 1)
                            if not first:
                                dve.wait_ge(y_added, NT * e - NT + t + 1)
                            nc.vector.scalar_tensor_tensor(out=acc[:, t, :], in0=p_y[(b + t) % 2][0:TP, 0:F],
                                                           scalar=weight[:, t, bass.ds(e, 1)], in1=acc[:, t, :],
                                                           op0=ALU.mult, op1=ALU.add).then_inc(y_added, 1)

                    split_lo(0, 0)
                    split_lo(0, 1)
                    hidden_lo(0, 0)
                    hidden_lo(0, 1)
                    add(0, 0, first=True)
                    with dve.Fori(1, NE // 2) as i:
                        split_lo(i, 0)
                        hidden_lo(i, 0)
                        add(i - 1, 1)
                        split_lo(i, 1)
                        hidden_lo(i, 1)
                        add(i, 0)
                    add(NE // 2 - 1, 1)

                @block.tensor
                def _(pe):
                    def first_product(i, b, first=False):
                        e = 2 * i + b
                        pe.wait_ge(we_lo, 2 * e + 2)
                        n = 0
                        for m in range(KH):
                            for lo, up in HALF:
                                if not (first and n < 2):
                                    pe.wait_ge(hid_ok, NH * e + n - 1)
                                q = 0
                                for k in range(KF):
                                    for wp, dp in PASSES:
                                        last = nc.tensor.matmul(p_h[n % 2][:, 0:up - lo],
                                                                w1e[b][wp][:, k, m * P:(m + 1) * P],
                                                                xnT_hl[dp][:, k, lo:up], start=q == 0, stop=q == 5)
                                        q += 1
                                last.then_inc(h_psum, 1)
                                n += 1

                    def second_product(i, b, first=False):
                        e = 2 * i + b
                        pe.wait_ge(h_split, NH * e + NH)
                        for t in range(NT):
                            if not (first and t < 2):
                                pe.wait_ge(y_added, NT * e + t - 1)
                            q = 0
                            for k in range(KH):
                                for wp, dp in PASSES:
                                    last = nc.tensor.matmul(p_y[(b + t) % 2][0:TP, 0:F],
                                                            hT_hl[b][dp][:, k, t * TP:(t + 1) * TP],
                                                            w2e[b][wp][:, k, :], start=q == 0,
                                                            stop=q == 3 * KH - 1)
                                    q += 1
                            last.then_inc(y_psum, 1)

                    first_product(0, 0, first=True)
                    first_product(0, 1)
                    second_product(0, 0, first=True)
                    with pe.Fori(1, NE // 2) as i:
                        first_product(i, 0)
                        second_product(i - 1, 1)
                        first_product(i, 1)
                        second_product(i, 0)
                    second_product(NE // 2 - 1, 1)


_INS = ["x", "src", "dst", "edge_attr_256", "L0_gnn_W1f", "L0_gnn_b1f", "L0_gnn_W2f", "L0_gnn_b2f", "L0_gnn_W1m",
        "L0_gnn_b1m", "L0_gnn_W2m", "L0_gnn_b2m", "L0_gnn_g_int", "L0_gnn_beta_int", "L0_gnn_g_bn",
        "L0_gnn_beta_bn", "L0_ffn_Wg", "L0_ffn_bg", "L0_ffn_bias", "L0_ffn_W1", "L0_ffn_b1", "L0_ffn_W2",
        "L0_ffn_b2"]


def kernel(**inputs):
    import numpy as _np
    import concourse.bacc as _bacc
    from concourse import mybir as _mybir
    from concourse.bass_utils import run_bass_kernel_spmd as _run

    nc = _bacc.Bacc("TRN2", target_bir_lowering=False, num_devices=1)
    arrays, args = {}, []
    for name in _INS:
        a = _np.ascontiguousarray(inputs[name])
        arrays[f"in_{name}_dram"] = a
        args.append(nc.dram_tensor(f"in_{name}_dram", a.shape, _mybir.dt.from_np(a.dtype), kind="ExternalInput").ap())
    out = nc.dram_tensor("out_0_dram", inputs["x"].shape, _mybir.dt.float32, kind="ExternalOutput").ap()
    gnn_moe(nc, *args, out)
    r = _run(nc, [arrays], core_ids=[0])
    return r.results[0]["out_0_dram"]
```

```python
from contextlib import ExitStack

import concourse.bass as bass
from concourse import mybir

F32 = mybir.dt.float32
F32R = mybir.dt.float32r
I32 = mybir.dt.int32
ALU = mybir.AluOpType
ACT = mybir.ActivationFunctionType
AX_X = mybir.AxisListType.X

P = 128


def gnn_moe(nc, x, src, dst, edge_attr, W1f, b1f, W2f, b2f, W1m, b1m, W2m, b2m,
            g_int, beta_int, g_bn, beta_bn, Wg, bg, bias, W1, b1, W2, b2, out):
    N, F = x.shape
    E = edge_attr.shape[0]
    NE, _, H = W1.shape
    TP = 125
    NT = N // TP
    T = 4
    G = T * TP
    NG = E // G
    NPAIR = NG // 2
    KF = F // P
    KH = H // P
    F2 = 2 * F
    C = F2 // P
    EPS = 1e-5
    assert N == NT * TP and E == NG * G and NG % 2 == 0 and F == KF * P and F2 <= 512
    NPAD = N + N % 2
    HALF = [(0, 314), (314, NPAD)]
    PASSES = ((0, 0), (0, 1), (1, 0))

    table_dst = nc.dram_tensor("table_dst", (N, F2), F32, kind="Internal").ap()
    table_src = nc.dram_tensor("table_src", (N, F2), F32, kind="Internal").ap()
    z_gate = nc.dram_tensor("z_gate", (F, E), F32, kind="Internal").ap()
    z_val = nc.dram_tensor("z_val", (F, E), F32, kind="Internal").ap()

    ea_v = edge_attr.rearrange("(g p i) f -> g p i f", p=TP, i=T)
    src_v = src.rearrange("(g p i) -> g p i", p=TP, i=T)
    dst_v = dst.rearrange("(g p i) -> g p i", p=TP, i=T)
    zg_v = z_gate.rearrange("(j p) (g e) -> g p j e", p=P, e=G)
    zv_v = z_val.rearrange("(j p) (g e) -> g p j e", p=P, e=G)
    x_v = x.rearrange("(t p) f -> p t f", p=TP)
    out_v = out.rearrange("(t p) f -> p t f", p=TP)

    def column(v):
        return v.rearrange("(k p) -> p k", p=P)

    def spread(v, n):
        return v.rearrange("(a f) -> a f", a=1).broadcast_to((TP, n))

    whole = ExitStack()
    with whole:
        def sb(stack, name, shape, dt=F32, side="left"):
            return stack.enter_context(nc.sbuf_tensor(name, shape, dt, side=side))

        def ps(stack, name, shape, dt=F32):
            return stack.enter_context(nc.psum_tensor(name, shape, dt))

        def sems(stack, *names):
            return [stack.enter_context(nc.semaphore(n)) for n in names]

        x_sb = sb(whole, "x_sb", [TP, NT, F])
        xln = sb(whole, "xln", [TP, NT, F])
        ident = sb(whole, "ident", [P, P])
        ln_stats = sb(whole, "ln_stats", [TP, NT, 6])
        ln_mv = sb(whole, "ln_mv", [TP, NT, 2])
        ln_std = sb(whole, "ln_std", [TP, NT])
        gate_stats = sb(whole, "gate_stats", [P, KF, NG * 6])
        vecs = sb(whole, "vecs", [P, 4, KF])
        dst_stored, src_stored, v_in, w1_split, w2_split = sems(
            whole, "dst_stored", "src_stored", "v_in", "w1_split", "w2_split")
        ea_in = sems(whole, "ea_in0", "ea_in1")
        idx_in = sems(whole, "idx_in0", "idx_in1")
        got_dst = sems(whole, "got_dst0", "got_dst1")
        got_both = sems(whole, "got_both0", "got_both1")

        edge_mem = ExitStack()
        w1raw = sb(edge_mem, "w1raw", [P, KF, F2], side="right")
        w2raw = sb(edge_mem, "w2raw", [P, C, F], side="right")
        w1_hl = [sb(edge_mem, f"w1_{n}", [P, KF, F2], F32R, side="right") for n in ("hi", "lo")]
        w2_hl = [sb(edge_mem, f"w2_{n}", [P, C, F], F32R, side="right") for n in ("hi", "lo")]
        ea = [sb(edge_mem, f"ea{b}", [TP, T, F], side="right") for b in range(2)]
        idx = [sb(edge_mem, f"idx{b}", [TP, 2, T], I32, side="right") for b in range(2)]
        pre = [sb(edge_mem, f"pre{b}", [TP, T, F2], side="right") for b in range(2)]
        eaT_hl = [sb(edge_mem, f"eaT_{n}", [P, KF, G], F32R, side="right") for n in ("hi", "lo")]
        h_full = [sb(edge_mem, f"h_full{b}", [P, G], side="right") for b in range(2)]
        h_hl = [sb(edge_mem, f"h_{n}", [P, C, G], F32R, side="right") for n in ("hi", "lo")]
        zg_st = sb(edge_mem, "zg_st", [P, KF, G], side="right")
        zv_st = sb(edge_mem, "zv_st", [P, KF, G], side="right")

        def load_edges(sp, g, b):
            sp.dma_start(idx[b][:, 0, :], dst_v[g]).then_inc(idx_in[b], 16)
            sp.dma_start(idx[b][:, 1, :], src_v[g]).then_inc(idx_in[b], 16)
            sp.dma_start(ea[b][:], ea_v[g]).then_inc(ea_in[b], 16)

        def gather_dst(pool, b):
            pool.wait_ge(dst_stored, 16 * NT)
            for t in range(T):
                pool.indirect_dma_start(pre[b][:, t, :], None, table_dst, bass.IndirectOffsetOnAxis(
                    ap=idx[b][:, 0, t:t + 1], axis=0)).then_inc(got_dst[b], 16)

        def add_src(pool, b):
            pool.wait_ge(src_stored, 16 * NT)
            for t in range(T):
                pool.indirect_dma_start(pre[b][:, t, :], None, table_src, bass.IndirectOffsetOnAxis(
                    ap=idx[b][:, 1, t:t + 1], axis=0), compute_op=ALU.add).then_inc(got_both[b], 16)

        with ExitStack() as s:
            w1ab = sb(s, "w1ab", [P, 2, KF, F2])
            w1ab_hl = [sb(s, f"w1ab_{n}", [P, 2, KF, F2], F32R) for n in ("hi", "lo")]
            b1_bc = sb(s, "b1_bc", [TP, F2])
            xT_hl = [sb(s, f"xT_{n}", [P, KF, N], F32R) for n in ("hi", "lo")]
            rows = [sb(s, f"rows_{n}", [TP, NT, F2]) for n in ("dst", "src")]
            p_xT = [ps(s, f"p_xT{b}", [P, 512])[:, 0:KF * TP].rearrange("p (k n) -> p k n", k=KF)
                    for b in range(4)]
            p_row = [ps(s, f"p_row{b}", [P, 512])[0:TP] for b in range(4)]
            (x_in, w_in, b_in, w_in2, zeroed, ident_ok, dve_done, std_ok, xln_ok, xT_psum, xT_hi, xT_lo, wab_hi,
             wab_lo, row_psum, dst_ok, src_ok) = sems(
                s, "x_in", "w_in", "b_in", "w_in2", "zeroed", "ident_ok", "dve_done", "std_ok", "xln_ok",
                "xT_psum", "xT_hi_s", "xT_lo_s", "wab_hi", "wab_lo", "row_psum", "dst_ok", "src_ok")
            with nc.Block() as block:

                @block.sync
                def _(sp):
                    sp.dma_start(x_sb[:], x_v).then_inc(x_in, 16)
                    for b, w in enumerate((W1f, W1m)):
                        sp.dma_start(w1ab[:, :, :, b * F:(b + 1) * F], w[0:2 * F, :].rearrange(
                            "(a k p) n -> p a k n", a=2, p=P)).then_inc(w_in, 16)
                    for b, v in enumerate((b1f, b1m)):
                        sp.dma_start(b1_bc[:, b * F:(b + 1) * F], spread(v, F)).then_inc(b_in, 16)
                    load_edges(sp, 0, 0)
                    for b, w in enumerate((W1f, W1m)):
                        sp.dma_start(w1raw[:, :, b * F:(b + 1) * F],
                                     w[2 * F:3 * F, :].rearrange("(k p) n -> p k n", p=P)).then_inc(w_in2, 16)
                    for b, w in enumerate((W2f, W2m)):
                        sp.dma_start(w2raw[:, b * KF:(b + 1) * KF, :],
                                     w.rearrange("(k p) n -> p k n", p=P)).then_inc(w_in2, 16)
                    for t in range(NT):
                        sp.wait_ge(dst_ok, t + 1)
                        sp.dma_start(table_dst[t * TP:(t + 1) * TP, :], rows[0][:, t, :]).then_inc(dst_stored, 16)
                    load_edges(sp, 1, 1)
                    for n, v in enumerate((g_int, beta_int, b2f, b2m)):
                        sp.dma_start(vecs[:, n, :], column(v), allow_slow_non_contiguous=True).then_inc(v_in, 16)
                    for t in range(NT):
                        sp.wait_ge(src_ok, t + 1)
                        sp.dma_start(table_src[t * TP:(t + 1) * TP, :], rows[1][:, t, :]).then_inc(src_stored, 16)

                @block.gpsimd
                def _(pool):
                    nc.gpsimd.memset(ident[:], 0.0).then_inc(zeroed, 1)
                    pool.wait_ge(zeroed, 1)
                    nc.gpsimd.affine_select(out=ident[:], in_=ident[:], compare_op=ALU.not_equal, fill=1.0,
                                            base=0, pattern=[[-1, P]], channel_multiplier=1).then_inc(ident_ok, 1)
                    pool.wait_ge(idx_in[0], 32)
                    gather_dst(pool, 0)

                @block.vector
                def _(dve):
                    dve.wait_ge(x_in, 16)
                    for t in range(NT):
                        nc.vector.bn_stats(ln_stats[:, t, :], x_sb[:, t, :]).then_inc(dve_done, 1)
                    for t in range(NT):
                        dve.wait_ge(dve_done, t + 1)
                        nc.vector.bn_aggr(ln_mv[:, t, :], ln_stats[:, t, :]).then_inc(dve_done, 1)
                    dve.wait_ge(dve_done, 2 * NT)
                    nc.vector.tensor_scalar(ln_std[:], ln_mv[:, :, 1], EPS, None, ALU.add).then_inc(dve_done, 1)
                    dve.wait_ge(std_ok, 1)
                    nc.vector.reciprocal(ln_std[:], ln_std[:]).then_inc(dve_done, 1)
                    dve.wait_ge(dve_done, 2 * NT + 2)
                    for t in range(NT):
                        nc.vector.tensor_scalar(xln[:, t, :], x_sb[:, t, :], ln_mv[:, t, 0:1], ln_std[:, t:t + 1],
                                                ALU.subtract, ALU.mult).then_inc(xln_ok, 1)

                    def weights_lo(a):
                        dve.wait_ge(wab_hi, a + 1)
                        nc.vector.tensor_tensor(w1ab_hl[1][:, a], w1ab[:, a], w1ab_hl[0][:, a],
                                                ALU.subtract).then_inc(wab_lo, 1)

                    weights_lo(0)
                    for t in range(NT):
                        dve.wait_ge(xT_hi, t + 1)
                        nc.vector.tensor_tensor(xT_hl[1][:, :, t * TP:(t + 1) * TP], p_xT[t % 4],
                                                xT_hl[0][:, :, t * TP:(t + 1) * TP], ALU.subtract).then_inc(xT_lo, 1)
                    weights_lo(1)
                    dve.wait_ge(b_in, 32)
                    for t in range(NT):
                        dve.wait_ge(row_psum, t + 1)
                        nc.vector.tensor_tensor(rows[0][:, t, :], p_row[t % 4], b1_bc[:], ALU.add).then_inc(dst_ok, 1)
                    dve.wait_ge(w1_split, 1)
                    nc.vector.tensor_tensor(w1_hl[1][:], w1raw[:], w1_hl[0][:], ALU.subtract).then_inc(w1_split, 1)
                    dve.wait_ge(w2_split, 1)
                    nc.vector.tensor_tensor(w2_hl[1][:], w2raw[:], w2_hl[0][:], ALU.subtract).then_inc(w2_split, 1)

                @block.scalar
                def _(act):
                    act.wait_ge(dve_done, 2 * NT + 1)
                    nc.scalar.activation(ln_std[:], ln_std[:], ACT.Sqrt).then_inc(std_ok, 1)
                    act.wait_ge(w_in, 32)
                    nc.scalar.copy(w1ab_hl[0][:, 0], w1ab[:, 0]).then_inc(wab_hi, 1)
                    for t in range(NT):
                        act.wait_ge(xT_psum, t + 1)
                        nc.scalar.copy(xT_hl[0][:, :, t * TP:(t + 1) * TP], p_xT[t % 4]).then_inc(xT_hi, 1)
                    nc.scalar.copy(w1ab_hl[0][:, 1], w1ab[:, 1]).then_inc(wab_hi, 1)
                    act.wait_ge(w_in2, 64)
                    nc.scalar.copy(w1_hl[0][:], w1raw[:]).then_inc(w1_split, 1)
                    nc.scalar.copy(w2_hl[0][:], w2raw[:]).then_inc(w2_split, 1)
                    for t in range(NT):
                        act.wait_ge(row_psum, NT + t + 1)
                        nc.scalar.copy(rows[1][:, t, :], p_row[(NT + t) % 4]).then_inc(src_ok, 1)

                @block.tensor
                def _(pe):
                    pe.wait_ge(ident_ok, 1)
                    for t in range(NT):
                        pe.wait_ge(xln_ok, t + 1)
                        if t >= 4:
                            pe.wait_ge(xT_lo, t - 3)
                        for k in range(KF):
                            last = nc.tensor.transpose(p_xT[t % 4][:, k, :], xln[:, t, k * P:(k + 1) * P],
                                                       ident[0:TP, 0:TP])
                        last.then_inc(xT_psum, 1)
                    for a in range(2):
                        pe.wait_ge(wab_lo, a + 1)
                        for t in range(NT):
                            n = a * NT + t
                            if a == 0:
                                pe.wait_ge(xT_lo, t + 1)
                            if 4 <= n < NT + 4:
                                pe.wait_ge(dst_ok, n - 3)
                            elif n >= NT + 4:
                                pe.wait_ge(src_ok, n - NT - 3)
                            q = 0
                            for k in range(KF):
                                for wp, dp in PASSES:
                                    last = nc.tensor.matmul(p_row[n % 4], xT_hl[dp][:, k, t * TP:(t + 1) * TP],
                                                            w1ab_hl[wp][:, a, k, :], start=q == 0, stop=q == 5)
                                    q += 1
                            last.then_inc(row_psum, 1)

        gate = [sb(whole, f"gate{b}", [P, KF, G]) for b in range(4)]
        val = [sb(whole, f"val{b}", [P, KF, G]) for b in range(4)]
        didx = [sb(whole, f"didx{b}", [TP, T], I32) for b in range(4)]
        active = sb(whole, "active", [1, NG * NT], I32)
        raw1 = [sb(whole, f"raw1_{b}", [P, KF, H]) for b in range(2)]
        raw2 = [sb(whole, f"raw2_{b}", [P, KH, F]) for b in range(2)]
        w1e = [[sb(whole, f"w1e{b}_{n}", [P, KF, H], F32R) for n in ("hi", "lo")] for b in range(2)]
        w2e = [[sb(whole, f"w2e{b}_{n}", [P, KH, F], F32R) for n in ("hi", "lo")] for b in range(2)]
        z_in = sems(whole, *(f"z_in{b}" for b in range(4)))
        raw_in = sems(whole, "raw_in0", "raw_in1")
        active_in, w1e_hi, w1e_lo, w2e_hi, w2e_lo = sems(whole, "active_in", "w1e_hi", "w1e_lo", "w2e_hi", "w2e_lo")

        def load_z(sp, g, b):
            sp.dma_start(didx[b][:], dst_v[g]).then_inc(z_in[b], 16)
            sp.dma_start(gate[b][:], zg_v[g]).then_inc(z_in[b], 16)
            sp.dma_start(val[b][:], zv_v[g]).then_inc(z_in[b], 16)

        def load_expert(sp, e, b):
            sp.dma_start(raw1[b][:], W1[e].rearrange("(k p) n -> p k n", p=P)).then_inc(raw_in[b], 16)
            sp.dma_start(raw2[b][:], W2[e].rearrange("(k p) n -> p k n", p=P)).then_inc(raw_in[b], 16)

        with ExitStack() as s:
            dst_rows = sb(s, "dst_rows", [NG, G], I32)
            dst_f = sb(s, "dst_f", [NG, G])
            above = sb(s, "above", [NG, G])
            count = sb(s, "count", [NG, NT + 1])
            active_col = sb(s, "active_col", [NG, NT], I32)
            p_eaT = [ps(s, f"p_eaT{b}", [P, 512]) for b in range(KF)]
            p_pre = [ps(s, f"p_pre{b}", [P, 512]) for b in range(2)]
            p_hT = [ps(s, f"p_hT{b}", [P, 512]) for b in range(2)]
            p_z = [ps(s, f"p_z{b}", [P, 512]) for b in range(KF)]
            (dst_in, counted, active_ok, eaT_psum, eaT_hi, eaT_lo, pre_psum, pre_ok, hT_psum, silu_ok, h_lo_ok,
             zg_psum, zv_psum, zg_copied, zg_stats, zv_copied, zg_stored, zv_stored, gather_free) = sems(
                s, "dst_in", "counted", "active_ok", "eaT_psum", "eaT_hi_s", "eaT_lo_s", "pre_psum", "pre_ok",
                "hT_psum", "silu_ok", "h_lo_ok", "zg_psum", "zv_psum", "zg_copied", "zg_stats", "zv_copied",
                "zg_stored", "zv_stored", "gather_free")
            with nc.Block() as block:

                @block.sync
                def _(sp):
                    sp.dma_start(dst_rows[:], dst.rearrange("(g e) -> g e", e=G)).then_inc(dst_in, 16)

                    def step(i, b, first=False, last=False):
                        g = 2 * i + b
                        if not last:
                            sp.wait_ge(eaT_psum, KF * g + KF)
                            sp.wait_ge(got_both[b], 16 * T * i + 16 * T)
                            load_edges(sp, g + 2, b)
                        if not (first and b == 0):
                            sp.wait_ge(zv_copied, KF * g)
                            sp.dma_start(zv_v[g - 1], zv_st[:]).then_inc(zv_stored, 16)
                        sp.wait_ge(zg_copied, KF * g + KF)
                        sp.dma_start(zg_v[g], zg_st[:]).then_inc(zg_stored, 16)

                    for b in range(2):
                        step(0, b, first=True)
                    for b in range(2):
                        load_expert(sp, b, b)
                    with sp.Fori(1, NPAIR - 1) as i:
                        for b in range(2):
                            step(i, b)
                    sp.wait_ge(zg_stored, 16 * 4)
                    sp.wait_ge(zv_stored, 16 * 4)
                    for b in range(4):
                        load_z(sp, b, b)
                    for b in range(2):
                        step(NPAIR - 1, b, last=True)
                        if b == 0:
                            sp.wait_ge(active_ok, 1)
                            sp.dma_start(active[:].rearrange("a (g n) -> a g n", n=NT),
                                         active_col[:]).then_inc(active_in, 16)
                    sp.wait_ge(zv_copied, KF * NG)
                    sp.dma_start(zv_v[NG - 1], zv_st[:]).then_inc(zv_stored, 16)
                    sp.wait_ge(zv_stored, 16 * NG)
                    sp.wait_ge(zg_stored, 16 * NG)

                @block.gpsimd
                def _(pool):
                    def free_and_landed(i, b, first=False):
                        pool.wait_ge(idx_in[b], 32 * i + 32)
                        if not first:
                            pool.wait_ge(hT_psum, C * (2 * i + b) - C)
                        pool.sem_inc(gather_free, 1)

                    def add(i, b):
                        pool.wait_ge(got_dst[b], 16 * T * i + 16 * T)
                        pool.sem_inc(gather_free, 1)
                        add_src(pool, b)

                    add(0, 0)
                    free_and_landed(0, 1, first=True)
                    gather_dst(pool, 1)
                    add(0, 1)
                    with pool.Fori(1, NPAIR) as i:
                        for b in range(2):
                            free_and_landed(i, b)
                            gather_dst(pool, b)
                            add(i, b)

                @block.scalar
                def _(act):
                    act.wait_ge(v_in, 64)

                    def ea_hi(g, first=False):
                        for k in range(KF):
                            act.wait_ge(eaT_psum, KF * g + k + 1)
                            if not first:
                                act.wait_ge(pre_psum, T * g)
                            nc.scalar.copy(eaT_hl[0][:, k, :], p_eaT[k][:, 0:G]).then_inc(eaT_hi, 1)

                    def silu(g, branch, first):
                        for c in range(branch * KF, branch * KF + KF):
                            act.wait_ge(hT_psum, C * g + c + 1)
                            if not (first and c < 2):
                                act.wait_ge(h_lo_ok, C * g + c - 1)
                            if not first:
                                act.wait_ge(zv_psum if branch else zg_psum, KF * g)
                            nc.scalar.activation(h_hl[0][:, c, :], p_hT[c % 2][:, 0:G], ACT.Silu)
                            nc.scalar.activation(h_full[c % 2][:], p_hT[c % 2][:, 0:G],
                                                 ACT.Silu).then_inc(silu_ok, 1)

                    def store_values(g, first=False):
                        for j in range(KF):
                            act.wait_ge(zv_psum, KF * g + j + 1)
                            if not first:
                                act.wait_ge(zv_stored, 16 * g)
                            nc.scalar.activation(zv_st[:, j, :], p_z[j][:, 0:G], ACT.Identity,
                                                 bias=vecs[:, 3, j:j + 1]).then_inc(zv_copied, 1)

                    def step(i, b, first=False, last=False):
                        g = 2 * i + b
                        first, second, last = first and b == 0, first and b == 1, last and b == 1
                        silu(g, 0, first)
                        if not last:
                            ea_hi(g + 1)
                        if not first:
                            store_values(g - 1, first=second)
                        silu(g, 1, first)
                        for j in range(KF):
                            act.wait_ge(zg_psum, KF * g + j + 1)
                            if not first:
                                act.wait_ge(zg_stored, 16 * g)
                                act.wait_ge(zg_stats, KF * g)
                            nc.scalar.copy(zg_st[:, j, :], p_z[j][:, 0:G]).then_inc(zg_copied, 1)

                    ea_hi(0, first=True)
                    for b in range(2):
                        step(0, b, first=True)
                    with act.Fori(1, NPAIR - 1) as i:
                        for b in range(2):
                            step(i, b)
                    for b in range(2):
                        step(NPAIR - 1, b, last=True)
                        act.wait_ge(raw_in[b], 32)
                        nc.scalar.copy(w1e[b][0][:], raw1[b][:]).then_inc(w1e_hi, 1)
                        nc.scalar.copy(w2e[b][0][:], raw2[b][:]).then_inc(w2e_hi, 1)
                    store_values(NG - 1)

                @block.vector
                def _(dve):
                    def find_active():
                        dve.wait_ge(dst_in, 16)
                        nc.vector.tensor_copy(dst_f[:], dst_rows[:]).then_inc(counted, 1)
                        dve.wait_ge(counted, 1)
                        for n in range(NT + 1):
                            nc.vector.tensor_scalar(above[:], dst_f[:], float(n * TP), None,
                                                    ALU.is_ge).then_inc(counted, 1)
                            dve.wait_ge(counted, 2 * n + 2)
                            nc.vector.tensor_reduce(count[:, n:n + 1], above[:], AX_X, ALU.add).then_inc(counted, 1)
                            dve.wait_ge(counted, 2 * n + 3)
                        nc.vector.tensor_tensor(active_col[:], count[:, 0:NT], count[:, 1:NT + 1],
                                                ALU.subtract).then_inc(active_ok, 1)

                    def split_expert(b):
                        dve.wait_ge(w1e_hi, b + 1)
                        nc.vector.tensor_tensor(w1e[b][1][:], raw1[b][:], w1e[b][0][:],
                                                ALU.subtract).then_inc(w1e_lo, 1)
                        dve.wait_ge(w2e_hi, b + 1)
                        nc.vector.tensor_tensor(w2e[b][1][:], raw2[b][:], w2e[b][0][:],
                                                ALU.subtract).then_inc(w2e_lo, 1)

                    def ea_lo(g):
                        for k in range(KF):
                            dve.wait_ge(eaT_hi, KF * g + k + 1)
                            nc.vector.tensor_tensor(eaT_hl[1][:, k, :], p_eaT[k][:, 0:G], eaT_hl[0][:, k, :],
                                                    ALU.subtract).then_inc(eaT_lo, 1)

                    def h_lo(g, branch):
                        for c in range(branch * KF, branch * KF + KF):
                            dve.wait_ge(silu_ok, C * g + c + 1)
                            nc.vector.tensor_tensor(h_hl[1][:, c, :], h_full[c % 2][:], h_hl[0][:, c, :],
                                                    ALU.subtract).then_inc(h_lo_ok, 1)

                    def step(i, b, last=False):
                        g = 2 * i + b
                        dve.wait_ge(got_both[b], 16 * T * i + 16 * T)
                        for t in range(T):
                            dve.wait_ge(pre_psum, T * g + t + 1)
                            nc.vector.tensor_tensor(pre[b][:, t, :], p_pre[t % 2][0:TP, :], pre[b][:, t, :],
                                                    ALU.add).then_inc(pre_ok, 1)
                        h_lo(g, 0)
                        if not (last and b == 1):
                            ea_lo(g + 1)
                        h_lo(g, 1)
                        for j in range(KF):
                            dve.wait_ge(zg_copied, KF * g + j + 1)
                            nc.vector.bn_stats(gate_stats[:, j, bass.ds(g * 6, 6)],
                                               zg_st[:, j, :]).then_inc(zg_stats, 1)

                    ea_lo(0)
                    with dve.Fori(0, NPAIR - 1) as i:
                        for b in range(2):
                            step(i, b)
                    find_active()
                    for b in range(2):
                        step(NPAIR - 1, b, last=True)
                        split_expert(b)

                @block.tensor
                def _(pe):
                    def transpose_ea(g, i, b):
                        pe.wait_ge(ea_in[b], 16 * i + 16)
                        for k in range(KF):
                            for t in range(T):
                                last = nc.tensor.transpose(p_eaT[k][:, t * TP:(t + 1) * TP],
                                                           ea[b][:, t, k * P:(k + 1) * P], ident[0:TP, 0:TP])
                            last.then_inc(eaT_psum, 1)

                    def first_layer(g, first):
                        pe.wait_ge(eaT_hi, KF * g + KF)
                        pe.wait_ge(eaT_lo, KF * g + KF)
                        for t in range(T):
                            if not (first and t < 2):
                                pe.wait_ge(pre_ok, T * g + t - 1)
                            n = 0
                            for k in range(KF):
                                for wp, dp in PASSES:
                                    last = nc.tensor.matmul(p_pre[t % 2][0:TP, :],
                                                            eaT_hl[dp][:, k, t * TP:(t + 1) * TP],
                                                            w1_hl[wp][:, k, :], start=n == 0, stop=n == 5)
                                    n += 1
                            last.then_inc(pre_psum, 1)

                    def transpose_pre(g, b, branch, first):
                        pe.wait_ge(pre_ok, T * g + T)
                        for c in range(branch * KF, branch * KF + KF):
                            if not (first and c < 2):
                                pe.wait_ge(silu_ok, C * g + c - 1)
                            for t in range(T):
                                last = nc.tensor.transpose(p_hT[c % 2][:, t * TP:(t + 1) * TP],
                                                           pre[b][:, t, c * P:(c + 1) * P], ident[0:TP, 0:TP])
                            last.then_inc(hT_psum, 1)

                    def second_layer(g, branch, first=False):
                        pe.wait_ge(h_lo_ok, C * g + branch * KF + KF)
                        for j in range(KF):
                            if branch:
                                pe.wait_ge(zg_copied, KF * g + j + 1)
                            elif not first:
                                pe.wait_ge(zv_copied, KF * g - KF + j + 1)
                            n = 0
                            for k in range(KF):
                                for wp, dp in PASSES:
                                    c = branch * KF + k
                                    last = nc.tensor.matmul(p_z[j][:, 0:G], w2_hl[wp][:, c, j * P:(j + 1) * P],
                                                            h_hl[dp][:, c, :], start=n == 0, stop=n == 5)
                                    n += 1
                            last.then_inc(zv_psum if branch else zg_psum, 1)

                    def step(i, b, first=False, last=False):
                        g = 2 * i + b
                        first, last = first and b == 0, last and b == 1
                        first_layer(g, first)
                        if not last:
                            transpose_ea(g + 1, i + b, 1 - b)
                        transpose_pre(g, b, 0, first)
                        if not first:
                            second_layer(g - 1, 1)
                        transpose_pre(g, b, 1, first)
                        second_layer(g, 0, first)

                    transpose_ea(0, 0, 0)
                    pe.wait_ge(w1_split, 2)
                    pe.wait_ge(w2_split, 2)
                    for b in range(2):
                        step(0, b, first=True)
                    with pe.Fori(1, NPAIR - 1) as i:
                        for b in range(2):
                            step(i, b)
                    for b in range(2):
                        step(NPAIR - 1, b, last=True)
                    second_layer(NG - 1, 1)

        edge_mem.close()

        agg = sb(whole, "agg", [TP, NT, F])
        with ExitStack() as s:
            mv = sb(s, "mv", [P, KF, 2])
            tmp = sb(s, "tmp", [P, 4, KF])
            dstf = [sb(s, f"dstf{b}", [TP, T]) for b in range(2)]
            msgT = [sb(s, f"msgT{b}", [P, KF, G]) for b in range(2)]
            msg = [sb(s, f"msg{b}", [TP, T, 2, F], F32R) for b in range(2)]
            onehot = [sb(s, f"onehot{b}", [TP, T, N], F32R) for b in range(2)]
            node_id = sb(s, "node_id", [TP, N])
            zeros = sb(s, "zeros", [TP, F2])
            zeros_r = sb(s, "zeros_r", [TP, F2], F32R)
            p_msg = [ps(s, f"p_msg{h}", [P, 2, F]) for h in range(T // 2)]
            p_agg = [ps(s, f"p_agg{n}", [TP, 2, F]) for n in range(NT)]
            (ids_ok, chain, std2_ok, bn_ok, zero_ok, gate_ok, msgT0_ok, msgT1_ok, msg_psum, msg_hi, msg_lo, dstf_ok,
             onehot_free, summed, agg_hi_ok, agg_ok) = sems(
                s, "ids_ok", "chain", "std2_ok", "bn_ok", "zero_ok", "gate_ok", "msgT0_ok", "msgT1_ok", "msg_psum",
                "msg_hi", "msg_lo", "dstf_ok", "onehot_free", "summed", "agg_hi_ok", "agg_ok")
            NQUAD = NG // 4
            with nc.Block() as block:

                def groups(eng, step):
                    for b in range(4):
                        step(0, b, first=True)
                    with eng.Fori(1, NQUAD - 1) as i:
                        for b in range(4):
                            step(i, b)
                    for b in range(4):
                        step(NQUAD - 1, b, last=True)

                @block.sync
                def _(sp):
                    with sp.Fori(1, NQUAD) as i:
                        for b in range(4):
                            g = 4 * i + b
                            sp.wait_ge(dstf_ok, g - 3)
                            sp.dma_start(didx[b][:], dst_v[g]).then_inc(z_in[b], 16)
                            sp.wait_ge(msgT0_ok, g - 3)
                            sp.dma_start(gate[b][:, 0, :], zg_v[g, :, 0]).then_inc(z_in[b], 16)
                            sp.dma_start(val[b][:, 0, :], zv_v[g, :, 0]).then_inc(z_in[b], 16)
                            sp.wait_ge(msgT1_ok, g - 3)
                            sp.dma_start(gate[b][:, 1, :], zg_v[g, :, 1]).then_inc(z_in[b], 16)
                            sp.dma_start(val[b][:, 1, :], zv_v[g, :, 1]).then_inc(z_in[b], 16)

                def z_landed(i, first):
                    return 48 if first else 80 * i + 48

                def message(eng, j, i, b, done):
                    eng.wait_ge(gate_ok, KF * (4 * i + b) + j + 1)
                    eng.tensor_tensor(msgT[b % 2][:, j, :], val[b][:, j, :], gate[b][:, j, :],
                                      ALU.mult).then_inc(done, 1)

                @block.gpsimd
                def _(pool):
                    nc.gpsimd.iota(node_id[:], pattern=[[1, N]], base=0, channel_multiplier=0,
                                   allow_small_or_imprecise_dtypes=True).then_inc(ids_ok, 1)

                    def step(i, b, first=False, last=False):
                        g = 4 * i + b
                        if not (first and b < 2):
                            pool.wait_ge(msg_psum, 2 * g - 2)
                        message(pool, 1, i, b, msgT1_ok)

                    groups(pool, step)

                @block.scalar
                def _(act):
                    act.wait_ge(chain, 2)
                    nc.scalar.activation(tmp[:, 0, :], tmp[:, 0, :], ACT.Sqrt).then_inc(std2_ok, 1)
                    act.wait_ge(bn_ok, 1)

                    def sigmoid(i, b, first=False):
                        act.wait_ge(z_in[b], z_landed(i, first))
                        for j in range(KF):
                            nc.scalar.activation(gate[b][:, j, :], gate[b][:, j, :], ACT.Sigmoid,
                                                 bias=tmp[:, 3, j:j + 1],
                                                 scale=tmp[:, 1, j:j + 1]).then_inc(gate_ok, 1)

                    def step(i, b, first=False, last=False):
                        g = 4 * i + b
                        if b < 3:
                            sigmoid(i, b + 1, first)
                        elif not last:
                            sigmoid(i + 1, 0)
                        for h in range(T // 2):
                            act.wait_ge(msg_psum, 2 * g + h + 1)
                            nc.scalar.copy(msg[b % 2][:, 2 * h:2 * h + 2, 0, :], p_msg[h][0:TP]).then_inc(msg_hi, 1)

                    sigmoid(0, 0, first=True)
                    groups(act, step)
                    for n in range(NT):
                        act.wait_ge(summed, 1)
                        nc.scalar.copy(agg[:, n, :], p_agg[n][:, 0, :]).then_inc(agg_hi_ok, 1)

                @block.vector
                def _(dve):
                    for j in range(KF):
                        last = nc.vector.bn_aggr(mv[:, j, :], gate_stats[:, j, :])
                    last.then_inc(chain, 1)
                    dve.wait_ge(chain, 1)
                    nc.vector.tensor_scalar(tmp[:, 0, :], mv[:, :, 1], EPS, None, ALU.add).then_inc(chain, 1)
                    nc.vector.memset(zeros[:], 0.0).then_inc(zero_ok, 1)
                    dve.wait_ge(zero_ok, 1)
                    nc.vector.tensor_copy(zeros_r[:], zeros[:]).then_inc(zero_ok, 1)
                    dve.wait_ge(std2_ok, 1)
                    nc.vector.reciprocal(tmp[:, 1, :], tmp[:, 0, :]).then_inc(chain, 1)
                    dve.wait_ge(chain, 3)
                    nc.vector.tensor_tensor(tmp[:, 1, :], tmp[:, 1, :], vecs[:, 0, :], ALU.mult).then_inc(chain, 1)
                    nc.vector.tensor_tensor(tmp[:, 2, :], mv[:, :, 0], vecs[:, 2, :], ALU.add).then_inc(chain, 1)
                    dve.wait_ge(chain, 5)
                    nc.vector.tensor_tensor(tmp[:, 2, :], vecs[:, 2, :], tmp[:, 2, :],
                                            ALU.subtract).then_inc(chain, 1)
                    dve.wait_ge(chain, 6)
                    nc.vector.tensor_tensor(tmp[:, 3, :], tmp[:, 2, :], tmp[:, 1, :], ALU.mult).then_inc(chain, 1)
                    dve.wait_ge(chain, 7)
                    nc.vector.tensor_tensor(tmp[:, 3, :], tmp[:, 3, :], vecs[:, 1, :], ALU.add).then_inc(bn_ok, 1)

                    flags = [[dve.alloc_register(f"dve_active{b}_{n}") for n in range(NT)] for b in range(2)]

                    def step(i, b, first=False, last=False):
                        g = 4 * i + b
                        if not (last and b == 3):
                            dve.load(flags[1 - b % 2], active[:, bass.ds((g + 1) * NT, NT)])
                            if not (first and b == 0):
                                dve.wait_ge(msg_psum, 2 * g)
                            message(dve, 0, i + (b == 3), (b + 1) % 4, msgT0_ok)
                        nc.vector.tensor_copy(dstf[b % 2][:], didx[b][:]).then_inc(dstf_ok, 1)
                        dve.wait_ge(msg_psum, 2 * g + 1)
                        dve.wait_ge(dstf_ok, g + 1)
                        dve.sem_inc(onehot_free, 1)
                        for n in range(NT):
                            with dve.If_ne(flags[b % 2][n], 0):
                                ids = node_id[:, n * TP:(n + 1) * TP].rearrange(
                                    "p (a n) -> p a n", a=1).broadcast_to((TP, T, TP))
                                dsts = dstf[b % 2][:].rearrange("p (t a) -> p t a", a=1).broadcast_to((TP, T, TP))
                                nc.vector.tensor_tensor(onehot[b % 2][:, :, n * TP:(n + 1) * TP], ids, dsts,
                                                        ALU.is_equal)
                        for h in range(T // 2):
                            dve.wait_ge(msg_hi, 2 * g + h + 1)
                            nc.vector.tensor_tensor(msg[b % 2][:, 2 * h:2 * h + 2, 1, :], p_msg[h][0:TP],
                                                    msg[b % 2][:, 2 * h:2 * h + 2, 0, :],
                                                    ALU.subtract).then_inc(msg_lo, 1)

                    dve.wait_ge(ids_ok, 1)
                    dve.wait_ge(active_in, 16)
                    dve.load(flags[0], active[:, 0:NT])
                    message(dve, 0, 0, 0, msgT0_ok)
                    groups(dve, step)
                    for n in range(NT):
                        dve.wait_ge(agg_hi_ok, n + 1)
                        nc.vector.tensor_tensor(agg[:, n, :], p_agg[n][:, 1, :], agg[:, n, :],
                                                ALU.add).then_inc(agg_ok, 1)

                @block.tensor
                def _(pe):
                    flags = [[pe.alloc_register(f"pe_active{b}_{n}") for n in range(NT)] for b in range(2)]

                    def transpose_msg(g, b, first=False):
                        pe.wait_ge(msgT0_ok, g + 1)
                        pe.wait_ge(msgT1_ok, g + 1)
                        for h in range(T // 2):
                            if not first:
                                pe.wait_ge(msg_lo, 2 * g - 1 + h)
                            for t in (2 * h, 2 * h + 1):
                                for j in range(KF):
                                    last = nc.tensor.transpose(p_msg[h][0:TP, t % 2, j * P:(j + 1) * P],
                                                               msgT[b % 2][:, j, t * TP:(t + 1) * TP], ident[:])
                            last.then_inc(msg_psum, 1)

                    def scatter(g, b):
                        pe.wait_ge(msg_lo, 2 * g + 2)
                        for n in range(NT):
                            with pe.If_ne(flags[b % 2][n], 0):
                                for t in range(T):
                                    nc.tensor.matmul(p_agg[n][:], onehot[b % 2][:, t, n * TP:(n + 1) * TP],
                                                     msg[b % 2][:, t, :, :], start=False, stop=False)

                    def step(i, b, first=False, last=False):
                        g = 4 * i + b
                        if not (first and b == 0):
                            transpose_msg(g, b)
                            pe.load(flags[b % 2], active[:, bass.ds(g * NT, NT)])
                            scatter(g - 1, b - 1)

                    pe.wait_ge(zero_ok, 2)
                    for n in range(NT):
                        nc.tensor.matmul(p_agg[n][:], zeros_r[:, 0:TP], zeros_r[:], start=True, stop=False)
                    pe.wait_ge(active_in, 16)
                    pe.load(flags[0], active[:, 0:NT])
                    transpose_msg(0, 0, first=True)
                    groups(pe, step)
                    scatter(NG - 1, 3)
                    for n in range(NT):
                        last = nc.tensor.matmul(p_agg[n][:], zeros_r[:, 0:TP], zeros_r[:], start=False, stop=True)
                    last.then_inc(summed, 1)

        with ExitStack() as s:
            NH = 2 * KH
            acc = sb(s, "acc", [TP, NT, F])
            weight = sb(s, "weight", [TP, NT, NE])
            xnT = sb(s, "xnT", [P, KF, NPAD])
            xnT_hl = [sb(s, f"xnT_{n}", [P, KF, NPAD], F32R) for n in ("hi", "lo")]
            b1T = sb(s, "b1T", [P, NE * KH])
            ones = sb(s, "ones", [TP, TP])
            bn_rows = sb(s, "bn_rows", [TP, 2, F])
            gate_b = sb(s, "gate_b", [TP, 2, NE])
            dev = sb(s, "dev", [TP, NT, F])
            sq = sb(s, "sq", [TP, NT, F])
            rs = sb(s, "rs", [TP, F])
            warm = sb(s, "warm", [TP, 1])
            wg_sb = sb(s, "wg_sb", [P, KF, NE])
            b1_sb = sb(s, "b1_sb", [NE * KH, P])
            b2_sb = sb(s, "b2_sb", [NE, F])
            expert_id = sb(s, "expert_id", [TP, NT, NE])
            rt = sb(s, "rt", [TP, 5, NT, NE])
            rs1 = sb(s, "rs1", [TP, 8, NT])
            wT = sb(s, "wT", [NE, NT, TP])
            b1e = [sb(s, f"b1e{b}", [P, KH]) for b in range(2)]
            hid = [sb(s, f"hid{b}", [P, 314]) for b in range(4)]
            hT_hl = [[sb(s, f"hT{b}_{n}", [P, KH, NPAD], F32R) for n in ("hi", "lo")] for b in range(2)]
            p_h = [ps(s, f"p_h{b}", [P, 512]) for b in range(4)]
            p_y = [ps(s, f"p_y{b}", [P, 512])[0:TP, 0:F] for b in range(2)]
            p_a = ps(s, "p_a", [P, 512])
            p_b = ps(s, "p_b", [P, 512])
            p_sum, p_var = p_h[0][0:TP, 0:F], p_h[1][0:TP, 0:F]
            p_xnT = [p_h[2 + b][:, 0:KF * TP].rearrange("p (k n) -> p k n", k=KF) for b in range(2)]
            p_log = p_b[0:TP, 0:NT * NE].rearrange("p (t e) -> p t e", t=NT)
            (n_in, ids2_ok, ones_ok, chain2, pre_add, dev_ok, sum_psum, sq_ok, var_psum, std3_ok, std4_ok, warm_ok,
             x1_ok, xn_ok, xnT_psum, xnT_hi, xnT_lo, log_psum, log_ok, exp_ok, weight_ok, wT_psum, wT_ok,
             b1_psum, b1T_ok, b2_psum, b2_ok, pad_ok, h_psum, hid_ok, h_split, y_psum, y_added, out_in,
             bias_ok) = sems(
                s, "n_in", "ids2_ok", "ones_ok", "chain2", "pre_add", "dev_ok", "sum_psum", "sq_ok", "var_psum",
                "std3_ok", "std4_ok", "warm_ok", "x1_ok", "xn_ok", "xnT_psum", "xnT_hi_s", "xnT_lo_s", "log_psum",
                "log_ok", "exp_ok", "weight_ok", "wT_psum", "wT_ok", "b1_psum", "b1T_ok", "b2_psum",
                "b2_ok", "pad_ok", "h_psum", "hid_ok", "h_split", "y_psum", "y_added", "out_in", "bias_ok")
            logit, pick1, pick2, pen, rest = (rt[:, n] for n in range(5))
            top1, top2, diff, expd, id1, id2, w1st, w2nd = (rs1[:, n, :] for n in range(8))

            def over_experts(v):
                return v.rearrange("p (t a) -> p t a", a=1).broadcast_to((TP, NT, NE))

            def over_nodes(v):
                return v.rearrange("p (a e) -> p a e", a=1).broadcast_to((TP, NT, NE))

            with nc.Block() as block:

                @block.sync
                def _(sp):
                    for n, v in enumerate((g_bn, beta_bn)):
                        sp.dma_start(bn_rows[:, n, :], spread(v, F)).then_inc(n_in, 16)
                    for n, v in enumerate((bg, bias)):
                        sp.dma_start(gate_b[:, n, :], spread(v, NE)).then_inc(n_in, 16)
                    sp.dma_start(wg_sb[:], Wg.rearrange("(k p) e -> p k e", p=P)).then_inc(n_in, 16)
                    sp.dma_start(b1_sb[:], b1.rearrange("e (m p) -> (e m) p", p=P)).then_inc(n_in, 16)
                    sp.dma_start(b2_sb[:], b2).then_inc(n_in, 16)
                    with sp.Fori(1, NE // 2) as i:
                        for b in range(2):
                            e = 2 * i + b
                            sp.wait_ge(w1e_lo, e - 1)
                            sp.dma_start(raw1[b][:], W1[e].rearrange("(k p) n -> p k n", p=P)).then_inc(
                                raw_in[b], 16)
                            sp.wait_ge(w2e_lo, e - 1)
                            sp.dma_start(raw2[b][:], W2[e].rearrange("(k p) n -> p k n", p=P)).then_inc(
                                raw_in[b], 16)
                    for t in range(NT):
                        sp.wait_ge(y_added, NT * NE - NT + t + 1)
                        sp.dma_start(out_v[:, t, :], acc[:, t, :]).then_inc(out_in, 16)
                    sp.wait_ge(out_in, 16 * NT)

                @block.gpsimd
                def _(pool):
                    pool.wait_ge(n_in, 16 * 7)
                    for t in range(NT):
                        nc.gpsimd.tensor_tensor(xln[:, t, :], xln[:, t, :], bn_rows[:, 1, :],
                                                ALU.add).then_inc(pre_add, 1)
                    nc.gpsimd.iota(expert_id[:], pattern=[[0, NT], [1, NE]], base=0, channel_multiplier=0,
                                   allow_small_or_imprecise_dtypes=True).then_inc(ids2_ok, 1)

                @block.scalar
                def _(act):
                    act.wait_ge(ones_ok, 2)
                    nc.scalar.activation(warm[:], warm[:], ACT.Sqrt).then_inc(warm_ok, 1)
                    for t in range(NT):
                        act.wait_ge(dev_ok, t + 1)
                        nc.scalar.activation(sq[:, t, :], dev[:, t, :], ACT.Square).then_inc(sq_ok, 1)
                    act.wait_ge(chain2, 1)
                    nc.scalar.activation(rs[:], rs[:], ACT.Sqrt).then_inc(std3_ok, 1)
                    act.wait_ge(std4_ok, 1)
                    nc.scalar.activation(ln_std[:], ln_std[:], ACT.Sqrt).then_inc(std4_ok, 1)
                    act.wait_ge(pad_ok, 2)
                    nc.scalar.copy(xnT_hl[0][:, :, N:NPAD], xnT[:, :, N:NPAD]).then_inc(pad_ok, 1)
                    for t in range(NT):
                        act.wait_ge(xnT_psum, t + 1)
                        nc.scalar.copy(xnT_hl[0][:, :, t * TP:(t + 1) * TP], p_xnT[t % 2]).then_inc(xnT_hi, 1)
                        nc.scalar.copy(xnT[:, :, t * TP:(t + 1) * TP], p_xnT[t % 2]).then_inc(xnT_hi, 1)
                    act.wait_ge(b1T_ok, 1)
                    for b in range(2):
                        nc.scalar.copy(b1e[b][:], b1T[:, b * KH:(b + 1) * KH]).then_inc(bias_ok, 1)

                    def hidden(i, b, first=False, start=False):
                        e = 2 * i + b
                        act.wait_ge(bias_ok, e + 1)
                        for m in range(KH):
                            for q, (lo, up) in enumerate(HALF):
                                n = 2 * m + q
                                act.wait_ge(h_psum, NH * e + n + 1)
                                if not (start and n < 4):
                                    act.wait_ge(h_split, NH * e + n - 3)
                                if not first:
                                    act.wait_ge(y_psum, NT * (e - 1))
                                nc.scalar.activation(hT_hl[b][0][:, m, lo:up], p_h[n % 4][:, 0:up - lo], ACT.Relu,
                                                     bias=b1e[b][:, m:m + 1])
                                nc.scalar.activation(hid[n % 4][:, 0:up - lo], p_h[n % 4][:, 0:up - lo], ACT.Relu,
                                                     bias=b1e[b][:, m:m + 1]).then_inc(hid_ok, 1)

                    def split1(i, b):
                        e = 2 * i + b
                        act.wait_ge(raw_in[b], 32 * i + 32)
                        act.wait_ge(h_psum, NH * (e - 1))
                        nc.scalar.copy(w1e[b][0][:], raw1[b][:]).then_inc(w1e_hi, 1)
                        nc.scalar.copy(b1e[b][:], b1T[:, bass.ds(e * KH, KH)]).then_inc(bias_ok, 1)

                    def split2(i, b):
                        act.wait_ge(y_psum, NT * (2 * i + b - 1))
                        nc.scalar.copy(w2e[b][0][:], raw2[b][:]).then_inc(w2e_hi, 1)

                    hidden(0, 0, first=True, start=True)
                    act.wait_ge(log_ok, 1)
                    nc.scalar.activation(expd, diff, ACT.Exp).then_inc(exp_ok, 1)
                    hidden(0, 1, first=True)
                    split1(1, 0)
                    with act.Fori(1, NE // 2 - 1) as i:
                        hidden(i, 0)
                        split1(i, 1)
                        split2(i, 0)
                        hidden(i, 1)
                        split1(i + 1, 0)
                        split2(i, 1)
                    hidden(NE // 2 - 1, 0)
                    split1(NE // 2 - 1, 1)
                    split2(NE // 2 - 1, 0)
                    hidden(NE // 2 - 1, 1)
                    split2(NE // 2 - 1, 1)

                @block.vector
                def _(dve):
                    done = [0]

                    def then(ins):
                        done[0] += 1
                        ins.then_inc(chain2, 1)
                        dve.wait_ge(chain2, done[0])

                    nc.vector.memset(ones[:], 1.0).then_inc(ones_ok, 1)
                    nc.vector.memset(warm[:], 1.0).then_inc(ones_ok, 1)
                    nc.vector.memset(xnT[:, :, N:NPAD], 0.0).then_inc(pad_ok, 1)
                    dve.wait_ge(pad_ok, 1)
                    nc.vector.tensor_copy(xnT_hl[1][:, :, N:NPAD], xnT[:, :, N:NPAD]).then_inc(pad_ok, 1)
                    dve.wait_ge(sum_psum, 1)
                    for t in range(NT):
                        nc.vector.scalar_tensor_tensor(out=dev[:, t, :], in0=p_sum, scalar=-1.0 / N,
                                                       in1=agg[:, t, :], op0=ALU.mult, op1=ALU.add).then_inc(dev_ok, 1)
                    dve.wait_ge(var_psum, 1)
                    then(nc.vector.tensor_scalar(rs[:], p_var, 1.0 / N, EPS, ALU.mult, ALU.add))
                    dve.wait_ge(std3_ok, 1)
                    then(nc.vector.reciprocal(rs[:], rs[:]))
                    dve.wait_ge(n_in, 16 * 7)
                    then(nc.vector.tensor_tensor(rs[:], rs[:], bn_rows[:, 0, :], ALU.mult))
                    base = done[0]
                    dve.wait_ge(dev_ok, NT)
                    dve.wait_ge(sq_ok, NT)
                    for t in range(NT):
                        nc.vector.tensor_tensor(dev[:, t, :], dev[:, t, :], rs[:], ALU.mult).then_inc(chain2, 1)
                    for t in range(NT):
                        dve.wait_ge(chain2, base + t + 1)
                        dve.wait_ge(pre_add, t + 1)
                        nc.vector.tensor_tensor(dev[:, t, :], dev[:, t, :], xln[:, t, :], ALU.add).then_inc(chain2, 1)
                    for t in range(NT):
                        dve.wait_ge(chain2, base + NT + t + 1)
                        nc.vector.scalar_tensor_tensor(out=x_sb[:, t, :], in0=dev[:, t, :], scalar=0.0,
                                                       in1=x_sb[:, t, :], op0=ALU.max, op1=ALU.add).then_inc(x1_ok, 1)
                    for t in range(NT):
                        dve.wait_ge(x1_ok, t + 1)
                        nc.vector.bn_stats(ln_stats[:, t, :], x_sb[:, t, :]).then_inc(chain2, 1)
                    for t in range(NT):
                        dve.wait_ge(chain2, base + 2 * NT + t + 1)
                        nc.vector.bn_aggr(ln_mv[:, t, :], ln_stats[:, t, :]).then_inc(chain2, 1)
                    dve.wait_ge(chain2, base + 4 * NT)
                    done[0] = base + 4 * NT
                    nc.vector.tensor_scalar(ln_std[:], ln_mv[:, :, 1], EPS, None, ALU.add).then_inc(std4_ok, 1)
                    dve.wait_ge(std4_ok, 2)
                    then(nc.vector.reciprocal(ln_std[:], ln_std[:]))
                    for t in range(NT):
                        nc.vector.tensor_scalar(xln[:, t, :], x_sb[:, t, :], ln_mv[:, t, 0:1], ln_std[:, t:t + 1],
                                                ALU.subtract, ALU.mult).then_inc(xn_ok, 1)
                    dve.wait_ge(b1_psum, 1)
                    nc.vector.tensor_copy(b1T[:], p_a[:, 0:NE * KH]).then_inc(b1T_ok, 1)
                    for t in range(NT):
                        dve.wait_ge(xnT_hi, 2 * t + 2)
                        nc.vector.tensor_tensor(xnT_hl[1][:, :, t * TP:(t + 1) * TP], p_xnT[t % 2],
                                                xnT_hl[0][:, :, t * TP:(t + 1) * TP], ALU.subtract).then_inc(xnT_lo, 1)

                    def hidden_lo(i, b):
                        for m in range(KH):
                            for q, (lo, up) in enumerate(HALF):
                                n = 2 * m + q
                                dve.wait_ge(hid_ok, NH * (2 * i + b) + n + 1)
                                nc.vector.tensor_tensor(hT_hl[b][1][:, m, lo:up], hid[n % 4][:, 0:up - lo],
                                                        hT_hl[b][0][:, m, lo:up], ALU.subtract).then_inc(h_split, 1)

                    def split1(i, b):
                        dve.wait_ge(w1e_hi, 2 * i + b + 1)
                        nc.vector.tensor_tensor(w1e[b][1][:], raw1[b][:], w1e[b][0][:],
                                                ALU.subtract).then_inc(w1e_lo, 1)

                    def split2(i, b):
                        dve.wait_ge(w2e_hi, 2 * i + b + 1)
                        nc.vector.tensor_tensor(w2e[b][1][:], raw2[b][:], w2e[b][0][:],
                                                ALU.subtract).then_inc(w2e_lo, 1)

                    def add(i, b, first=False):
                        e = 2 * i + b
                        for t in range(NT):
                            dve.wait_ge(y_psum, NT * e + t + 1)
                            if not first:
                                dve.wait_ge(y_added, NT * e - NT + t + 1)
                            nc.vector.scalar_tensor_tensor(out=acc[:, t, :], in0=p_y[(b + t) % 2],
                                                           scalar=weight[:, t, bass.ds(e, 1)],
                                                           in1=x_sb[:, t, :] if first else acc[:, t, :],
                                                           op0=ALU.mult, op1=ALU.add).then_inc(y_added, 1)

                    def pick(table, top, number, chosen):
                        then(nc.vector.tensor_reduce(top, table, AX_X, ALU.max))
                        then(nc.vector.tensor_tensor(pen, table, over_experts(top), ALU.is_lt))
                        then(nc.vector.scalar_tensor_tensor(out=pen, in0=pen, scalar=float(NE), in1=expert_id[:],
                                                            op0=ALU.mult, op1=ALU.add))
                        then(nc.vector.tensor_reduce(number, pen, AX_X, ALU.min))
                        then(nc.vector.tensor_tensor(chosen, expert_id[:], over_experts(number), ALU.is_equal))

                    hidden_lo(0, 0)
                    dve.wait_ge(log_psum, 1)
                    dve.wait_ge(ids2_ok, 1)
                    then(nc.vector.tensor_tensor(logit, p_log, over_nodes(gate_b[:, 0, :]), ALU.add))
                    then(nc.vector.tensor_tensor(logit, logit, over_nodes(gate_b[:, 1, :]), ALU.add))
                    pick(logit, top1, id1, pick1)
                    then(nc.vector.scalar_tensor_tensor(out=rest, in0=pick1, scalar=-3.0e38, in1=logit,
                                                        op0=ALU.mult, op1=ALU.add))
                    pick(rest, top2, id2, pick2)
                    nc.vector.tensor_tensor(diff, top2, top1, ALU.subtract).then_inc(log_ok, 1)
                    hidden_lo(0, 1)
                    dve.wait_ge(exp_ok, 1)
                    then(nc.vector.tensor_scalar(w1st, expd, 1.0, None, ALU.add))
                    then(nc.vector.reciprocal(w1st, w1st))
                    then(nc.vector.tensor_tensor(w2nd, expd, w1st, ALU.mult))
                    then(nc.vector.tensor_tensor(pick1, pick1, over_experts(w1st), ALU.mult))
                    then(nc.vector.tensor_tensor(pick2, pick2, over_experts(w2nd), ALU.mult))
                    nc.vector.tensor_tensor(weight[:], pick1, pick2, ALU.add).then_inc(weight_ok, 1)
                    split1(1, 0)
                    dve.wait_ge(weight_ok, 1)
                    add(0, 0, first=True)
                    dve.wait_ge(wT_psum, 1)
                    nc.vector.tensor_copy(wT[:, 0:4, :], p_a[0:NE, 0:4 * TP].rearrange(
                        "e (t n) -> e t n", t=4)).then_inc(wT_ok, 1)
                    nc.vector.tensor_copy(wT[:, 4, :], p_b[0:NE, 0:TP]).then_inc(wT_ok, 1)
                    with dve.Fori(1, NE // 2 - 1) as i:
                        hidden_lo(i, 0)
                        split1(i, 1)
                        add(i - 1, 1)
                        split2(i, 0)
                        hidden_lo(i, 1)
                        split1(i + 1, 0)
                        add(i, 0)
                        split2(i, 1)
                    hidden_lo(NE // 2 - 1, 0)
                    split1(NE // 2 - 1, 1)
                    add(NE // 2 - 2, 1)
                    split2(NE // 2 - 1, 0)
                    hidden_lo(NE // 2 - 1, 1)
                    add(NE // 2 - 1, 0)
                    split2(NE // 2 - 1, 1)
                    before = NT * (NE - 1)
                    for t in range(NT):
                        dve.wait_ge(b2_psum, 1 + (t + 1) // 5)
                        dve.wait_ge(y_added, before)
                        bank = (p_a, p_b)[t // 2 % 2][0:TP, (t % 2) * F:(t % 2 + 1) * F]
                        nc.vector.tensor_tensor(acc[:, t, :], bank, acc[:, t, :], ALU.add).then_inc(b2_ok, 1)
                    dve.wait_ge(b2_ok, NT)
                    add(NE // 2 - 1, 1)

                @block.tensor
                def _(pe):
                    pe.wait_ge(ones_ok, 1)
                    for t in range(NT):
                        last = nc.tensor.matmul(p_sum, ones[:], agg[:, t, :], start=t == 0, stop=t == NT - 1)
                    last.then_inc(sum_psum, 1)
                    pe.wait_ge(n_in, 16 * 7)
                    nc.tensor.transpose(p_a[:, 0:NE * KH], b1_sb[:], ident[0:NE * KH, 0:NE * KH]).then_inc(
                        b1_psum, 1)
                    for t in range(NT):
                        pe.wait_ge(sq_ok, t + 1)
                        last = nc.tensor.matmul(p_var, ones[:], sq[:, t, :], start=t == 0, stop=t == NT - 1)
                    last.then_inc(var_psum, 1)
                    for t in range(NT):
                        pe.wait_ge(xn_ok, t + 1)
                        if t >= 2:
                            pe.wait_ge(xnT_lo, t - 1)
                        for k in range(KF):
                            last = nc.tensor.transpose(p_xnT[t % 2][:, k, :], xln[:, t, k * P:(k + 1) * P],
                                                       ident[0:TP, 0:TP])
                        last.then_inc(xnT_psum, 1)
                    def first_product(i, b, first=False):
                        e = 2 * i + b
                        pe.wait_ge(w1e_lo, e + 1)
                        for m in range(KH):
                            for h, (lo, up) in enumerate(HALF):
                                n = 2 * m + h
                                if not (first and n < 4):
                                    pe.wait_ge(hid_ok, NH * e + n - 3)
                                q = 0
                                for k in range(KF):
                                    for wp, dp in PASSES:
                                        last = nc.tensor.matmul(p_h[n % 4][:, 0:up - lo],
                                                                w1e[b][wp][:, k, m * P:(m + 1) * P],
                                                                xnT_hl[dp][:, k, lo:up], start=q == 0, stop=q == 5)
                                        q += 1
                                last.then_inc(h_psum, 1)

                    def second_product(i, b, first=False):
                        e = 2 * i + b
                        pe.wait_ge(w2e_lo, e + 1)
                        pe.wait_ge(h_split, NH * e + NH)
                        for t in range(NT):
                            if not (first and t < 2):
                                pe.wait_ge(y_added, NT * e + t - 1)
                            q = 0
                            for k in range(KH):
                                for wp, dp in PASSES:
                                    last = nc.tensor.matmul(p_y[(b + t) % 2],
                                                            hT_hl[b][dp][:, k, t * TP:(t + 1) * TP],
                                                            w2e[b][wp][:, k, :], start=q == 0,
                                                            stop=q == 3 * KH - 1)
                                    q += 1
                            last.then_inc(y_psum, 1)

                    pe.wait_ge(xnT_lo, NT)
                    pe.wait_ge(pad_ok, 3)
                    first_product(0, 0, first=True)
                    pe.wait_ge(xnT_hi, 2 * NT)
                    for t in range(NT):
                        for k in range(KF):
                            last = nc.tensor.matmul(p_log[:, t, :], xnT[:, k, t * TP:(t + 1) * TP], wg_sb[:, k, :],
                                                    start=k == 0, stop=k == KF - 1)
                    last.then_inc(log_psum, 1)
                    first_product(0, 1)
                    second_product(0, 0, first=True)
                    pe.wait_ge(weight_ok, 1)
                    pe.wait_ge(b1T_ok, 1)
                    for t in range(NT):
                        to = p_a[0:NE, t * TP:(t + 1) * TP] if t < 4 else p_b[0:NE, 0:TP]
                        last = nc.tensor.transpose(to, weight[:, t, :], ident[0:TP, 0:TP])
                    last.then_inc(wT_psum, 1)
                    with pe.Fori(1, NE // 2) as i:
                        first_product(i, 0)
                        second_product(i - 1, 1)
                        first_product(i, 1)
                        second_product(i, 0)
                    pe.wait_ge(wT_ok, 2)
                    for t in range(NT):
                        if t == 4:
                            pe.wait_ge(b2_ok, 2)
                        bank = (p_a, p_b)[t // 2 % 2][0:TP, (t % 2) * F:(t % 2 + 1) * F]
                        last = nc.tensor.matmul(bank, wT[:, t, :], b2_sb[:], start=True, stop=True)
                        if t >= 3:
                            last.then_inc(b2_psum, 1)
                    second_product(NE // 2 - 1, 1)


_INS = ["x", "src", "dst", "edge_attr_256", "L0_gnn_W1f", "L0_gnn_b1f", "L0_gnn_W2f", "L0_gnn_b2f", "L0_gnn_W1m",
        "L0_gnn_b1m", "L0_gnn_W2m", "L0_gnn_b2m", "L0_gnn_g_int", "L0_gnn_beta_int", "L0_gnn_g_bn",
        "L0_gnn_beta_bn", "L0_ffn_Wg", "L0_ffn_bg", "L0_ffn_bias", "L0_ffn_W1", "L0_ffn_b1", "L0_ffn_W2",
        "L0_ffn_b2"]


def kernel(**inputs):
    import numpy as _np
    import concourse.bacc as _bacc
    from concourse import mybir as _mybir
    from concourse.bass_utils import run_bass_kernel_spmd as _run

    nc = _bacc.Bacc("TRN2", target_bir_lowering=False, num_devices=1)
    arrays, args = {}, []
    for name in _INS:
        a = _np.ascontiguousarray(inputs[name])
        arrays[f"in_{name}_dram"] = a
        args.append(nc.dram_tensor(f"in_{name}_dram", a.shape, _mybir.dt.from_np(a.dtype), kind="ExternalInput").ap())
    out = nc.dram_tensor("out_0_dram", inputs["x"].shape, _mybir.dt.float32, kind="ExternalOutput").ap()
    gnn_moe(nc, *args, out)
    r = _run(nc, [arrays], core_ids=[0])
    return r.results[0]["out_0_dram"]
```

```python
from contextlib import ExitStack

import concourse.bass as bass
from concourse import mybir

F32 = mybir.dt.float32
F32R = mybir.dt.float32r
I32 = mybir.dt.int32
ALU = mybir.AluOpType
ACT = mybir.ActivationFunctionType
AX_X = mybir.AxisListType.X

P = 128


def gnn_moe(nc, x, src, dst, edge_attr, W1f, b1f, W2f, b2f, W1m, b1m, W2m, b2m,
            g_int, beta_int, g_bn, beta_bn, Wg, bg, bias, W1, b1, W2, b2, out):
    N, F = x.shape
    E = edge_attr.shape[0]
    NE, _, H = W1.shape
    TP = 125
    ROWS = ((0, TP // 16 * 16), (TP // 16 * 16, TP))
    NT = N // TP
    T = 4
    G = T * TP
    NG = E // G
    NQUAD = NG // 4
    KF = F // P
    KH = H // P
    F2 = 2 * F
    C = F2 // P
    EPS = 1e-5
    assert N == NT * TP and E == NG * G and NG % 4 == 0 and F == KF * P and F2 <= 512
    NPAD = N + N % 2
    HALF = [(0, 314), (314, NPAD)]
    PASSES = ((0, 0), (0, 1), (1, 0))

    table_dst = nc.dram_tensor("table_dst", (N, F2), F32, kind="Internal").ap()
    table_src = nc.dram_tensor("table_src", (N, F2), F32, kind="Internal").ap()
    z_gate = nc.dram_tensor("z_gate", (NG, P, KF, G), F32, kind="Internal").ap()
    h_val = nc.dram_tensor("h_val", (NG, P, KF, G), F32, kind="Internal").ap()

    ea_v = edge_attr.rearrange("(g p i) f -> g p i f", p=TP, i=T)
    src_v = src.rearrange("(g p i) -> g p i", p=TP, i=T)
    dst_v = dst.rearrange("(g p i) -> g p i", p=TP, i=T)
    x_v = x.rearrange("(t p) f -> p t f", p=TP)
    out_v = out.rearrange("(t p) f -> p t f", p=TP)

    def column(v):
        return v.rearrange("(k p) -> p k", p=P)

    def spread(v, n):
        return v.rearrange("(a f) -> a f", a=1).broadcast_to((TP, n))

    whole = ExitStack()
    with whole:
        def sb(stack, name, shape, dt=F32, side="left"):
            return stack.enter_context(nc.sbuf_tensor(name, shape, dt, side=side))

        def ps(stack, name, shape, dt=F32):
            return stack.enter_context(nc.psum_tensor(name, shape, dt))

        def sems(stack, *names):
            return [stack.enter_context(nc.semaphore(n)) for n in names]

        x_sb = sb(whole, "x_sb", [TP, NT, F])
        xln = sb(whole, "xln", [TP, NT, F])
        ident = sb(whole, "ident", [P, P])
        ln_stats = sb(whole, "ln_stats", [TP, NT, 6])
        ln_mv = sb(whole, "ln_mv", [TP, NT, 2])
        ln_std = sb(whole, "ln_std", [TP, NT])
        gate_stats = sb(whole, "gate_stats", [P, KF, NG * 6])
        vecs = sb(whole, "vecs", [P, 4, KF])
        dst_stored, src_stored, v_in, w1_split, w2_split = sems(
            whole, "dst_stored", "src_stored", "v_in", "w1_split", "w2_split")
        w2v_hl = [sb(whole, f"w2v_{n}", [P, KF, F], F32R) for n in ("hi", "lo")]
        ea_in = sems(whole, "ea_in0", "ea_in1")
        idx_in = sems(whole, *(f"idx_in{b}" for b in range(4)))
        got_dst = sems(whole, *(f"got_dst{b}" for b in range(4)))
        got_both = sems(whole, *(f"got_both{b}" for b in range(4)))

        dst_rows = sb(whole, "dst_rows", [NG, G], I32)
        warm = sb(whole, "warm", [TP, 1])
        zg_stored, hv_stored, hv_hi, hv_lo, dst_in = sems(
            whole, "zg_stored", "hv_stored", "hv_hi", "hv_lo", "dst_in")

        msg_mem = ExitStack()
        zg_st = sb(msg_mem, "zg_st", [P, KF, G], side="right")
        hv_st = sb(msg_mem, "hv_st", [P, KF, G], side="right")
        hvT_hl = [[sb(msg_mem, f"hvT{b}_{n}", [P, KF, G], F32R, side="right") for n in ("hi", "lo")]
                  for b in range(2)]
        edge_mem = ExitStack()
        w1_hl = [sb(edge_mem, f"w1_{n}", [P, KF, F2], F32R, side="right") for n in ("hi", "lo")]
        w2g_hl = [sb(edge_mem, f"w2g_{n}", [P, KF, F], F32R, side="right") for n in ("hi", "lo")]
        ea = [sb(edge_mem, f"ea{b}", [TP, T, F], side="right") for b in range(2)]
        idx = [sb(edge_mem, f"idx{b}", [TP, 2, T], I32, side="right") for b in range(4)]
        pre = [sb(edge_mem, f"pre{b}", [TP, T, F2], side="right") for b in range(4)]
        eaT_hl = [sb(edge_mem, f"eaT_{n}", [P, KF, G], F32R, side="right") for n in ("hi", "lo")]
        h_full = [sb(edge_mem, f"h_full{k}", [P, G], side="right") for k in range(KF)]
        h_hl = [[sb(edge_mem, f"h{b}_{n}", [P, KF, G], F32R, side="right") for n in ("hi", "lo")]
                for b in range(2)]

        def load_idx(sp, g, b):
            sp.dma_start(idx[b][:, 0, :], dst_v[g]).then_inc(idx_in[b], 16)
            sp.dma_start(idx[b][:, 1, :], src_v[g]).then_inc(idx_in[b], 16)

        def load_ea(sp, g, b):
            for lo, up in ROWS:
                sp.dma_start(ea[b][lo:up], ea_v[g, lo:up]).then_inc(ea_in[b], 16)

        def gather_dst(pool, b):
            pool.wait_ge(dst_stored, 32 * NT)
            for t in range(T):
                pool.indirect_dma_start(pre[b][:, t, :], None, table_dst, bass.IndirectOffsetOnAxis(
                    ap=idx[b][:, 0, t:t + 1], axis=0)).then_inc(got_dst[b], 16)

        def add_src(pool, b):
            pool.wait_ge(src_stored, 32 * NT)
            for t in range(T):
                pool.indirect_dma_start(pre[b][:, t, :], None, table_src, bass.IndirectOffsetOnAxis(
                    ap=idx[b][:, 1, t:t + 1], axis=0), compute_op=ALU.add).then_inc(got_both[b], 16)

        with ExitStack() as s:
            w1raw = sb(s, "w1raw", [P, KF, F2])
            w2raw = sb(s, "w2raw", [P, C, F])
            w1ab = sb(s, "w1ab", [P, 2, KF, F2])
            w1ab_hl = [sb(s, f"w1ab_{n}", [P, 2, KF, F2], F32R) for n in ("hi", "lo")]
            b1_bc = sb(s, "b1_bc", [TP, F2])
            xT_hl = [sb(s, f"xT_{n}", [P, KF, N], F32R) for n in ("hi", "lo")]
            rows = [sb(s, f"rows_{n}", [TP, NT, F2]) for n in ("dst", "src")]
            p_xT = [ps(s, f"p_xT{b}", [P, 512])[:, 0:KF * TP].rearrange("p (k n) -> p k n", k=KF)
                    for b in range(4)]
            p_row = [ps(s, f"p_row{b}", [P, 512])[0:TP] for b in range(4)]
            (x_in, b_in, w_in2, zeroed, ident_ok, dve_done, std_ok, xln_ok, xT_psum, xT_hi, xT_lo, wab_hi,
             wab_lo0, wab_lo, row_psum, dst_ok, src_ok) = sems(
                s, "x_in", "b_in", "w_in2", "zeroed", "ident_ok", "dve_done", "std_ok", "xln_ok",
                "xT_psum", "xT_hi_s", "xT_lo_s", "wab_hi", "wab_lo0", "wab_lo", "row_psum", "dst_ok", "src_ok")
            wab_in = sems(s, "wdst_in", "wsrc_in")
            with nc.Block(no_gpsimd_drain=True) as block:

                @block.sync
                def _(sp):
                    for lo, up in ROWS:
                        sp.dma_start(x_sb[lo:up], x_v[lo:up]).then_inc(x_in, 16)
                    for a in range(2):
                        for b, w in enumerate((W1f, W1m)):
                            sp.dma_start(w1ab[:, a, :, b * F:(b + 1) * F], w[a * F:(a + 1) * F, :].rearrange(
                                "(k p) n -> p k n", p=P)).then_inc(wab_in[a], 16)
                    for b, v in enumerate((b1f, b1m)):
                        sp.dma_start(b1_bc[:, b * F:(b + 1) * F], spread(v, F)).then_inc(b_in, 16)
                    load_idx(sp, 0, 0)
                    load_ea(sp, 0, 0)
                    for b, w in enumerate((W1f, W1m)):
                        sp.dma_start(w1raw[:, :, b * F:(b + 1) * F],
                                     w[2 * F:3 * F, :].rearrange("(k p) n -> p k n", p=P)).then_inc(w_in2, 16)
                    for b, w in enumerate((W2f, W2m)):
                        sp.dma_start(w2raw[:, b * KF:(b + 1) * KF, :],
                                     w.rearrange("(k p) n -> p k n", p=P)).then_inc(w_in2, 16)
                    load_ea(sp, 1, 1)
                    for b in range(1, 4):
                        load_idx(sp, b, b)
                    sp.dma_start(dst_rows[:], dst.rearrange("(g e) -> g e", e=G)).then_inc(dst_in, 16)
                    for n, v in enumerate((g_int, beta_int, b2f, b2m)):
                        sp.dma_start(vecs[:, n, :], column(v), allow_slow_non_contiguous=True).then_inc(v_in, 16)
                    for t in range(NT):
                        sp.wait_ge(dst_ok, t + 1)
                        for lo, up in ROWS:
                            sp.dma_start(table_dst[t * TP + lo:t * TP + up, :],
                                         rows[0][lo:up, t, :]).then_inc(dst_stored, 16)
                    for t in range(NT):
                        sp.wait_ge(src_ok, t + 1)
                        for lo, up in ROWS:
                            sp.dma_start(table_src[t * TP + lo:t * TP + up, :],
                                         rows[1][lo:up, t, :]).then_inc(src_stored, 16)

                @block.gpsimd
                def _(pool):
                    nc.gpsimd.memset(warm[:], 1.0)
                    nc.gpsimd.memset(ident[:], 0.0).then_inc(zeroed, 1)
                    pool.wait_ge(zeroed, 1)
                    nc.gpsimd.affine_select(out=ident[:], in_=ident[:], compare_op=ALU.not_equal, fill=1.0,
                                            base=0, pattern=[[-1, P]], channel_multiplier=1).then_inc(ident_ok, 1)
                    pool.wait_ge(wab_hi, 1)
                    nc.gpsimd.tensor_tensor(w1ab_hl[1][:, 0], w1ab[:, 0], w1ab_hl[0][:, 0],
                                            ALU.subtract).then_inc(wab_lo0, 1)
                    for b in range(2):
                        pool.wait_ge(idx_in[b], 32)
                        gather_dst(pool, b)

                @block.vector
                def _(dve):
                    dve.wait_ge(x_in, 32)
                    for t in range(NT):
                        nc.vector.bn_stats(ln_stats[:, t, :], x_sb[:, t, :]).then_inc(dve_done, 1)
                    for t in range(NT):
                        dve.wait_ge(dve_done, t + 1)
                        nc.vector.bn_aggr(ln_mv[:, t, :], ln_stats[:, t, :]).then_inc(dve_done, 1)
                    dve.wait_ge(dve_done, 2 * NT)
                    nc.vector.tensor_scalar(ln_std[:], ln_mv[:, :, 1], EPS, None, ALU.add).then_inc(dve_done, 1)
                    dve.wait_ge(std_ok, 1)
                    nc.vector.reciprocal(ln_std[:], ln_std[:]).then_inc(dve_done, 1)
                    dve.wait_ge(dve_done, 2 * NT + 2)
                    for t in range(NT):
                        nc.vector.tensor_scalar(xln[:, t, :], x_sb[:, t, :], ln_mv[:, t, 0:1], ln_std[:, t:t + 1],
                                                ALU.subtract, ALU.mult).then_inc(xln_ok, 1)

                    for t in range(NT):
                        dve.wait_ge(xT_hi, t + 1)
                        nc.vector.tensor_tensor(xT_hl[1][:, :, t * TP:(t + 1) * TP], p_xT[t % 4],
                                                xT_hl[0][:, :, t * TP:(t + 1) * TP], ALU.subtract).then_inc(xT_lo, 1)
                    dve.wait_ge(wab_hi, 2)
                    nc.vector.tensor_tensor(w1ab_hl[1][:, 1], w1ab[:, 1], w1ab_hl[0][:, 1],
                                            ALU.subtract).then_inc(wab_lo, 1)
                    dve.wait_ge(b_in, 32)
                    for t in range(NT):
                        dve.wait_ge(row_psum, t + 1)
                        nc.vector.tensor_tensor(rows[0][:, t, :], p_row[t % 4], b1_bc[:], ALU.add).then_inc(dst_ok, 1)
                    dve.wait_ge(w1_split, 1)
                    nc.vector.tensor_tensor(w1_hl[1][:], w1raw[:], w1_hl[0][:], ALU.subtract).then_inc(w1_split, 1)
                    dve.wait_ge(w2_split, 1)
                    nc.vector.tensor_tensor(w2g_hl[1][:], w2raw[:, 0:KF], w2g_hl[0][:],
                                            ALU.subtract).then_inc(w2_split, 1)
                    nc.vector.tensor_tensor(w2v_hl[1][:], w2raw[:, KF:C], w2v_hl[0][:],
                                            ALU.subtract).then_inc(w2_split, 1)

                @block.scalar
                def _(act):
                    act.wait_ge(dve_done, 2 * NT + 1)
                    nc.scalar.activation(ln_std[:], ln_std[:], ACT.Sqrt).then_inc(std_ok, 1)
                    act.wait_ge(wab_in[0], 32)
                    nc.scalar.copy(w1ab_hl[0][:, 0], w1ab[:, 0]).then_inc(wab_hi, 1)
                    for t in range(NT):
                        act.wait_ge(xT_psum, t + 1)
                        nc.scalar.copy(xT_hl[0][:, :, t * TP:(t + 1) * TP], p_xT[t % 4]).then_inc(xT_hi, 1)
                    act.wait_ge(wab_in[1], 32)
                    nc.scalar.copy(w1ab_hl[0][:, 1], w1ab[:, 1]).then_inc(wab_hi, 1)
                    act.wait_ge(w_in2, 64)
                    nc.scalar.copy(w1_hl[0][:], w1raw[:]).then_inc(w1_split, 1)
                    nc.scalar.copy(w2g_hl[0][:], w2raw[:, 0:KF])
                    nc.scalar.copy(w2v_hl[0][:], w2raw[:, KF:C]).then_inc(w2_split, 1)
                    act.wait_ge(ident_ok, 1)
                    nc.scalar.activation(warm[:], warm[:], ACT.Silu)
                    for t in range(NT):
                        act.wait_ge(row_psum, NT + t + 1)
                        nc.scalar.copy(rows[1][:, t, :], p_row[(NT + t) % 4]).then_inc(src_ok, 1)

                @block.tensor
                def _(pe):
                    pe.wait_ge(ident_ok, 1)
                    for t in range(NT):
                        pe.wait_ge(xln_ok, t + 1)
                        if t >= 4:
                            pe.wait_ge(xT_lo, t - 3)
                        for k in range(KF):
                            last = nc.tensor.transpose(p_xT[t % 4][:, k, :], xln[:, t, k * P:(k + 1) * P],
                                                       ident[0:TP, 0:TP])
                        last.then_inc(xT_psum, 1)
                    for a in range(2):
                        pe.wait_ge(wab_lo if a else wab_lo0, 1)
                        for t in range(NT):
                            n = a * NT + t
                            if a == 0:
                                pe.wait_ge(xT_lo, t + 1)
                            if 4 <= n < NT + 4:
                                pe.wait_ge(dst_ok, n - 3)
                            elif n >= NT + 4:
                                pe.wait_ge(src_ok, n - NT - 3)
                            q = 0
                            for k in range(KF):
                                for wp, dp in PASSES:
                                    last = nc.tensor.matmul(p_row[n % 4], xT_hl[dp][:, k, t * TP:(t + 1) * TP],
                                                            w1ab_hl[wp][:, a, k, :], start=q == 0, stop=q == 5)
                                    q += 1
                            last.then_inc(row_psum, 1)

        gate = [sb(whole, f"gate{b}", [P, KF, G]) for b in range(4)]
        hv = [sb(whole, f"hv{b}", [P, KF, G]) for b in range(4)]
        active = sb(whole, "active", [1, NG * NT], I32)
        dst_all = sb(whole, "dst_all", [TP, NG, T], I32)
        dst_num = sb(whole, "dst_num", [TP, NG, T])
        gate_in = sems(whole, *(f"gate_in{b}" for b in range(4)))
        hv_in = sems(whole, *(f"hv_in{b}" for b in range(4)))
        active_in, ids_ok = sems(whole, "active_in", "ids_ok")

        def load_gates(sp, g, b):
            sp.dma_start(gate[b][:], z_gate[g]).then_inc(gate_in[b], 16)

        def load_hidden(sp, g, b):
            sp.dma_start(hv[b][:], h_val[g]).then_inc(hv_in[b], 16)

        def hidden_hi(act, i, b):
            act.wait_ge(hv_in[b], 16 * i + 16)
            nc.scalar.copy(hvT_hl[b % 2][0][:], hv[b][:]).then_inc(hv_hi, 1)

        def split_hidden(pool, g, b):
            pool.wait_ge(hv_hi, g + 1)
            nc.gpsimd.tensor_tensor(hvT_hl[b % 2][1][:], hv[b][:], hvT_hl[b % 2][0][:],
                                    ALU.subtract).then_inc(hv_lo, 1)

        def groups(eng, step):
            for b in range(4):
                step(0, b, first=True)
            with eng.Fori(1, NQUAD - 1) as i:
                for b in range(4):
                    step(i, b)
            for b in range(4):
                step(NQUAD - 1, b, last=True)

        with ExitStack() as s:
            dst_f = sb(s, "dst_f", [NG, G])
            above = sb(s, "above", [NG, G])
            count = sb(s, "count", [NG, NT + 1])
            active_col = sb(s, "active_col", [NG, NT], I32)
            p_eaT = [ps(s, f"p_eaT{b}", [P, 512]) for b in range(KF)]
            p_pre = [ps(s, f"p_pre{b}", [P, 512]) for b in range(2)]
            p_hT = [ps(s, f"p_hT{b}", [P, 512]) for b in range(KF)]
            p_z = [ps(s, f"p_z{b}", [P, 512]) for b in range(KF)]
            (counted, active_ok, eaT_psum, eaT_hi, eaT_lo, pre_psum, pre_ok, hT_psum, silu_ok, h_lo_ok,
             hv_ok, zg_psum, zg_copied, zg_stats, gather_free) = sems(
                s, "counted", "active_ok", "eaT_psum", "eaT_hi_s", "eaT_lo_s", "pre_psum", "pre_ok",
                "hT_psum", "silu_ok", "h_lo_ok", "hv_ok", "zg_psum", "zg_copied", "zg_stats",
                "gather_free")

            def pre_bank(t, first):
                return (p_z[t - 2] if first and t >= 2 else p_pre[t % 2])[0:TP, :]

            with nc.Block(no_gpsimd_drain=True) as block:

                @block.sync
                def _(sp):
                    def store_gates(g):
                        sp.wait_ge(zg_copied, KF * g + KF)
                        sp.dma_start(z_gate[g], zg_st[:]).then_inc(zg_stored, 16)

                    def step(i, b, first=False, last=False):
                        g = 4 * i + b
                        if not last:
                            sp.wait_ge(got_both[b], 16 * T * (i + 1))
                            load_idx(sp, g + 4, b)
                        if not (last and b >= 2):
                            sp.wait_ge(eaT_psum, KF * g + KF)
                            load_ea(sp, g + 2, b % 2)
                        if not (first and b == 0):
                            store_gates(g - 1)
                        sp.wait_ge(hv_ok, KF * g + KF)
                        sp.dma_start(h_val[g], hv_st[:]).then_inc(hv_stored, 16)

                    for b in range(4):
                        step(0, b, first=True)
                    sp.dma_start(dst_all[:], dst.rearrange("(g p i) -> p g i", p=TP, i=T)).then_inc(dst_in, 16)
                    sp.wait_ge(active_ok, 1)
                    sp.dma_start(active[:].rearrange("a (g n) -> a g n", n=NT), active_col[:]).then_inc(active_in, 16)
                    with sp.Fori(1, NQUAD - 1) as i:
                        for b in range(4):
                            step(i, b)
                    sp.wait_ge(hv_stored, 16 * 4)
                    sp.wait_ge(zg_stored, 16 * 4)
                    for b in range(4):
                        load_hidden(sp, b, b)
                        load_gates(sp, b, b)
                        step(NQUAD - 1, b, last=True)
                    store_gates(NG - 1)

                @block.gpsimd
                def _(pool):
                    def add(i, b):
                        pool.wait_ge(got_dst[b], 16 * T * i + 16 * T)
                        pool.sem_inc(gather_free, 1)
                        add_src(pool, b)

                    def step(i, b, first=False, last=False):
                        g = 4 * i + b
                        if not (first and b == 0 or last and b == 3):
                            nb = (b + 1) % 4
                            pool.wait_ge(idx_in[nb], 32 * (i + (b == 3)) + 32)
                            if not (first and b < 3):
                                pool.wait_ge(hT_psum, C * (g - 2))
                            pool.sem_inc(gather_free, 1)
                            gather_dst(pool, nb)
                        if not (first and b < 2):
                            add(i, b)

                    for b in range(2):
                        add(0, b)
                    groups(pool, step)
                    for b in range(2):
                        split_hidden(pool, b, b)

                @block.scalar
                def _(act):
                    def ea_hi(g):
                        for k in range(KF):
                            act.wait_ge(eaT_psum, KF * g + k + 1)
                            nc.scalar.copy(eaT_hl[0][:, k, :], p_eaT[k][:, 0:G]).then_inc(eaT_hi, 1)

                    def copy_gates(g, first=False):
                        for j in range(KF):
                            act.wait_ge(zg_psum, KF * g + j + 1)
                            if not first:
                                act.wait_ge(zg_stored, 16 * g)
                                act.wait_ge(zg_stats, KF * g)
                            nc.scalar.copy(zg_st[:, j, :], p_z[j][:, 0:G]).then_inc(zg_copied, 1)

                    def step(i, b, first=False, last=False):
                        g = 4 * i + b
                        if not (last and b == 3):
                            ea_hi(g + 1)
                        for k in range(KF):
                            act.wait_ge(hT_psum, C * g + k + 1)
                            if not (first and b == 0):
                                act.wait_ge(h_lo_ok, KF * g - KF + k + 1)
                            if not (first and b < 2):
                                act.wait_ge(zg_psum, KF * g - KF)
                            nc.scalar.activation(h_hl[b % 2][0][:, k, :], p_hT[k][:, 0:G], ACT.Silu)
                            nc.scalar.activation(h_full[k][:], p_hT[k][:, 0:G], ACT.Silu).then_inc(silu_ok, 1)
                        if not (first and b == 0):
                            copy_gates(g - 1, first and b == 1)
                        for k in range(KF):
                            act.wait_ge(hT_psum, C * g + KF + k + 1)
                            if not (first and b == 0):
                                act.wait_ge(hv_stored, 16 * g)
                            nc.scalar.activation(hv_st[:, k, :], p_hT[k][:, 0:G], ACT.Silu).then_inc(hv_ok, 1)

                    ea_hi(0)
                    groups(act, step)
                    for b in range(2):
                        hidden_hi(act, 0, b)
                    copy_gates(NG - 1)

                @block.vector
                def _(dve):
                    def ea_lo(g):
                        for k in range(KF):
                            dve.wait_ge(eaT_hi, KF * g + k + 1)
                            nc.vector.tensor_tensor(eaT_hl[1][:, k, :], p_eaT[k][:, 0:G], eaT_hl[0][:, k, :],
                                                    ALU.subtract).then_inc(eaT_lo, 1)

                    def gate_statistics(g):
                        for j in range(KF):
                            dve.wait_ge(zg_copied, KF * g + j + 1)
                            nc.vector.bn_stats(gate_stats[:, j, bass.ds(g * 6, 6)],
                                               zg_st[:, j, :]).then_inc(zg_stats, 1)

                    def compare(n):
                        dve.wait_ge(counted, 2 * n + 1)
                        nc.vector.tensor_scalar(above[:], dst_f[:], float(n * TP), None,
                                                ALU.is_ge).then_inc(counted, 1)

                    def count_above(n):
                        dve.wait_ge(counted, 2 * n + 2)
                        nc.vector.tensor_reduce(count[:, n:n + 1], above[:], AX_X, ALU.add).then_inc(counted, 1)

                    def step(i, b, first=False, last=False):
                        g = 4 * i + b
                        dve.wait_ge(got_both[b], 16 * T * i + 16 * T)
                        for t in range(T):
                            dve.wait_ge(pre_psum, T * g + t + 1)
                            for cols in ((slice(0, F), slice(F, F2)) if t == T - 1 else (slice(0, F2),)):
                                nc.vector.tensor_tensor(pre[b][:, t, cols], pre_bank(t, first and b == 0)[:, cols],
                                                        pre[b][:, t, cols], ALU.add).then_inc(pre_ok, 1)
                            if first and b > 0:
                                (compare, count_above)[t % 2](2 * b - 2 + t // 2)
                        if not (last and b == 3):
                            ea_lo(g + 1)
                        for k in range(KF):
                            dve.wait_ge(silu_ok, KF * g + k + 1)
                            nc.vector.tensor_tensor(h_hl[b % 2][1][:, k, :], h_full[k][:], h_hl[b % 2][0][:, k, :],
                                                    ALU.subtract).then_inc(h_lo_ok, 1)
                        if first and b == 0:
                            dve.wait_ge(dst_in, 16)
                            nc.vector.tensor_copy(dst_f[:], dst_rows[:]).then_inc(counted, 1)
                        else:
                            gate_statistics(g - 1)
                        if first and b == 3:
                            dve.wait_ge(counted, 2 * NT + 3)
                            nc.vector.tensor_tensor(active_col[:], count[:, 0:NT], count[:, 1:NT + 1],
                                                    ALU.subtract).then_inc(active_ok, 1)

                    ea_lo(0)
                    groups(dve, step)
                    dve.wait_ge(dst_in, 32)
                    nc.vector.tensor_copy(dst_num[:], dst_all[:]).then_inc(ids_ok, 1)
                    gate_statistics(NG - 1)

                @block.tensor
                def _(pe):
                    def transpose_ea(g, i, b):
                        pe.wait_ge(ea_in[b % 2], 64 * i + 32 * (b // 2) + 32)
                        for k in range(KF):
                            for t in range(T):
                                last = nc.tensor.transpose(p_eaT[k][:, t * TP:(t + 1) * TP],
                                                           ea[b % 2][:, t, k * P:(k + 1) * P], ident[0:TP, 0:TP])
                            last.then_inc(eaT_psum, 1)

                    def first_layer(g, first):
                        pe.wait_ge(eaT_lo, KF * g + KF)
                        for t in range(T):
                            if t >= 2 and not first:
                                pe.wait_ge(pre_ok, (T + 1) * g + t - 1)
                            n = 0
                            for k in range(KF):
                                for wp, dp in PASSES:
                                    last = nc.tensor.matmul(pre_bank(t, first),
                                                            eaT_hl[dp][:, k, t * TP:(t + 1) * TP],
                                                            w1_hl[wp][:, k, :], start=n == 0, stop=n == 5)
                                    n += 1
                            last.then_inc(pre_psum, 1)

                    def transpose_pre(g, b, branch, first):
                        pe.wait_ge(pre_ok, (T + 1) * g + T + branch)
                        for k in range(KF):
                            c = branch * KF + k
                            if branch:
                                pe.wait_ge(silu_ok, KF * g + k + 1)
                            elif not first:
                                pe.wait_ge(hv_ok, KF * g - KF + k + 1)
                            for t in range(T):
                                last = nc.tensor.transpose(p_hT[k][:, t * TP:(t + 1) * TP],
                                                           pre[b][:, t, c * P:(c + 1) * P], ident[0:TP, 0:TP])
                            last.then_inc(hT_psum, 1)

                    def second_layer(g, par, first=False):
                        pe.wait_ge(h_lo_ok, KF * g + KF)
                        for j in range(KF):
                            if not first:
                                pe.wait_ge(zg_copied, KF * g - KF + j + 1)
                            n = 0
                            for k in range(KF):
                                for wp, dp in PASSES:
                                    last = nc.tensor.matmul(p_z[j][:, 0:G], w2g_hl[wp][:, k, j * P:(j + 1) * P],
                                                            h_hl[par][dp][:, k, :], start=n == 0, stop=n == 5)
                                    n += 1
                            last.then_inc(zg_psum, 1)

                    def step(i, b, first=False, last=False):
                        g = 4 * i + b
                        first_layer(g, first and b == 0)
                        if not (last and b == 3):
                            transpose_ea(g + 1, i + (b == 3), (b + 1) % 4)
                        transpose_pre(g, b, 0, first and b == 0)
                        if not (first and b == 0):
                            second_layer(g - 1, (b - 1) % 2, first and b == 1)
                        transpose_pre(g, b, 1, False)

                    transpose_ea(0, 0, 0)
                    pe.wait_ge(w1_split, 2)
                    pe.wait_ge(w2_split, 3)
                    groups(pe, step)
                    second_layer(NG - 1, 1)

        edge_mem.close()

        agg = sb(whole, "agg", [TP, NT, F])
        raw1 = [sb(whole, f"raw1_{b}", [P, KF, H]) for b in range(2)]
        raw2 = [sb(whole, f"raw2_{b}", [P, KH, F]) for b in range(2)]
        w1e = [[sb(whole, f"w1e{b}_{n}", [P, KF, H], F32R) for n in ("hi", "lo")] for b in range(2)]
        w2e = [[sb(whole, f"w2e{b}_{n}", [P, KH, F], F32R) for n in ("hi", "lo")] for b in range(2)]
        raw_in = sems(whole, "raw_in0", "raw_in1")
        w1e_hi, w1e_lo, w2e_hi, w2e_lo = sems(whole, "w1e_hi", "w1e_lo", "w2e_hi", "w2e_lo")

        def load_expert(sp, e, b):
            sp.dma_start(raw1[b][:], W1[e].rearrange("(k p) n -> p k n", p=P)).then_inc(raw_in[b], 16)
            sp.dma_start(raw2[b][:], W2[e].rearrange("(k p) n -> p k n", p=P)).then_inc(raw_in[b], 16)

        with ExitStack() as s:
            mv = sb(s, "mv", [P, KF, 2])
            tmp = sb(s, "tmp", [P, 4, KF])
            msgT = sb(s, "msgT", [P, KF, G])
            msg = sb(s, "msg", [TP, 2, T, F], F32R)
            onehot = [sb(s, f"onehot{b}", [TP, T, N], F32R) for b in range(2)]
            node_id = sb(s, "node_id", [TP, N])
            zeros = sb(s, "zeros", [TP, F2])
            zeros_r = sb(s, "zeros_r", [TP, F2], F32R)
            p_msg = [ps(s, f"p_msg{j}", [P, T, P]) for j in range(KF)]
            p_v = [ps(s, f"p_v{j}", [P, 512]) for j in range(KF)]
            p_agg = [ps(s, f"p_agg{n}", [TP, 2, F]) for n in range((NT + 1) // 2)]
            (chain, std2_ok, bn_ok, zero_ok, gate_ok, v_psum, msgT_ok, msg_psum,
             msg_hi, msg_lo, onehot_free, summed, agg_ok) = sems(
                s, "chain", "std2_ok", "bn_ok", "zero_ok", "gate_ok", "v_psum", "msgT_ok",
                "msg_psum", "msg_hi", "msg_lo", "onehot_free", "summed", "agg_ok")
            with nc.Block(no_gpsimd_drain=True) as block:

                @block.sync
                def _(sp):
                    sp.wait_ge(hv_stored, 16 * NG)
                    sp.wait_ge(zg_stored, 16 * NG)
                    with sp.Fori(1, NQUAD) as i:
                        for b in range(4):
                            g = 4 * i + b
                            sp.wait_ge(hv_lo, g - 3)
                            load_hidden(sp, g, b)
                            sp.wait_ge(msgT_ok, KF * (g - 3))
                            load_gates(sp, g, b)
                    for b in range(2):
                        load_expert(sp, b, b)

                @block.gpsimd
                def _(pool):
                    nc.gpsimd.iota(node_id[:], pattern=[[1, N]], base=0, channel_multiplier=0,
                                   allow_small_or_imprecise_dtypes=True).then_inc(ids_ok, 1)

                    def step(i, b, first=False, last=False):
                        if not (last and b >= 2):
                            split_hidden(pool, 4 * i + b + 2, (b + 2) % 4)
                        if last and b >= 2:
                            e = b - 2
                            pool.wait_ge(w1e_hi, e + 1)
                            nc.gpsimd.tensor_tensor(w1e[e][1][:], raw1[e][:], w1e[e][0][:],
                                                    ALU.subtract).then_inc(w1e_lo, 1)
                            pool.wait_ge(w2e_hi, e + 1)
                            nc.gpsimd.tensor_tensor(w2e[e][1][:], raw2[e][:], w2e[e][0][:],
                                                    ALU.subtract).then_inc(w2e_lo, 1)

                    groups(pool, step)

                @block.scalar
                def _(act):
                    def sigmoid(i, b):
                        act.wait_ge(gate_in[b], 16 * i + 16)
                        for j in range(KF):
                            nc.scalar.activation(gate[b][:, j, :], gate[b][:, j, :], ACT.Sigmoid,
                                                 bias=tmp[:, 3, j:j + 1],
                                                 scale=tmp[:, 1, j:j + 1]).then_inc(gate_ok, 1)

                    def step(i, b, first=False, last=False):
                        g = 4 * i + b
                        if not (last and b >= 2):
                            act.wait_ge(v_psum, KF * (g + 1))
                            hidden_hi(act, i + (b >= 2), (b + 2) % 4)
                        for j in range(KF):
                            act.wait_ge(msg_psum, KF * g + j + 1)
                            nc.scalar.copy(msg[:, 0, :, j * P:(j + 1) * P], p_msg[j][0:TP]).then_inc(msg_hi, 1)
                        if not (last and b == 3):
                            sigmoid(i + (b == 3), (b + 1) % 4)
                        if last:
                            act.wait_ge(raw_in[b // 2], 32)
                            if b % 2 == 0:
                                nc.scalar.copy(w1e[b // 2][0][:], raw1[b // 2][:]).then_inc(w1e_hi, 1)
                            else:
                                nc.scalar.copy(w2e[b // 2][0][:], raw2[b // 2][:]).then_inc(w2e_hi, 1)

                    nc.scalar.activation(warm[:], warm[:], ACT.Sqrt)
                    act.wait_ge(chain, 2)
                    nc.scalar.activation(tmp[:, 0, :], tmp[:, 0, :], ACT.Sqrt).then_inc(std2_ok, 1)
                    act.wait_ge(bn_ok, 1)
                    sigmoid(0, 0)
                    groups(act, step)
                    act.wait_ge(summed, 1)
                    nc.scalar.copy(agg[:, 0:2, :], p_agg[0][:]).then_inc(agg_ok, 1)

                @block.vector
                def _(dve):
                    dve.wait_ge(v_in, 64)
                    for j in range(KF):
                        last = nc.vector.bn_aggr(mv[:, j, :], gate_stats[:, j, :])
                    last.then_inc(chain, 1)
                    dve.wait_ge(chain, 1)
                    nc.vector.tensor_scalar(tmp[:, 0, :], mv[:, :, 1], EPS, None, ALU.add).then_inc(chain, 1)
                    nc.vector.tensor_tensor(tmp[:, 2, :], mv[:, :, 0], vecs[:, 2, :], ALU.add).then_inc(chain, 1)
                    dve.wait_ge(chain, 3)
                    nc.vector.tensor_tensor(tmp[:, 2, :], vecs[:, 2, :], tmp[:, 2, :],
                                            ALU.subtract).then_inc(chain, 1)
                    dve.wait_ge(std2_ok, 1)
                    nc.vector.reciprocal(tmp[:, 1, :], tmp[:, 0, :]).then_inc(chain, 1)
                    dve.wait_ge(chain, 5)
                    nc.vector.tensor_tensor(tmp[:, 1, :], tmp[:, 1, :], vecs[:, 0, :], ALU.mult).then_inc(chain, 1)
                    dve.wait_ge(chain, 6)
                    nc.vector.tensor_tensor(tmp[:, 3, :], tmp[:, 2, :], tmp[:, 1, :], ALU.mult).then_inc(chain, 1)
                    dve.wait_ge(chain, 7)
                    nc.vector.tensor_tensor(tmp[:, 3, :], tmp[:, 3, :], vecs[:, 1, :], ALU.add).then_inc(bn_ok, 1)
                    nc.vector.memset(zeros[:], 0.0).then_inc(zero_ok, 1)
                    dve.wait_ge(zero_ok, 1)
                    nc.vector.tensor_copy(zeros_r[:], zeros[:]).then_inc(zero_ok, 1)

                    flags = [dve.alloc_register(f"dve_active{n}") for n in range(NT)]

                    def message(j, g, b):
                        dve.wait_ge(v_psum, KF * g + j + 1)
                        dve.wait_ge(gate_ok, KF * g + j + 1)
                        nc.vector.scalar_tensor_tensor(out=msgT[:, j, :], in0=p_v[j][:, 0:G],
                                                       scalar=vecs[:, 3, j:j + 1], in1=gate[b][:, j, :],
                                                       op0=ALU.add, op1=ALU.mult).then_inc(msgT_ok, 1)

                    def one_hot(g, par):
                        for n in range(NT):
                            with dve.If_ne(flags[n], 0):
                                ids = node_id[:, n * TP:(n + 1) * TP].rearrange(
                                    "p (a n) -> p a n", a=1).broadcast_to((TP, T, TP))
                                dsts = dst_num[:, bass.ds(g, 1), :].rearrange(
                                    "p a t -> p t a").broadcast_to((TP, T, TP))
                                nc.vector.tensor_tensor(onehot[par][:, :, n * TP:(n + 1) * TP], ids, dsts,
                                                        ALU.is_equal)

                    def step(i, b, first=False, last=False):
                        g = 4 * i + b
                        for j in range(KF):
                            dve.wait_ge(msg_hi, KF * g + j + 1)
                            nc.vector.tensor_tensor(msg[:, 1, :, j * P:(j + 1) * P], p_msg[j][0:TP],
                                                    msg[:, 0, :, j * P:(j + 1) * P],
                                                    ALU.subtract).then_inc(msg_lo, 1)
                        if not (last and b == 3):
                            dve.load(flags, active[:, bass.ds((g + 1) * NT, NT)])
                            for j in range(KF):
                                message(j, g + 1, (b + 1) % 4)
                            one_hot(g + 1, (b + 1) % 2)

                    dve.wait_ge(ids_ok, 2)
                    dve.wait_ge(active_in, 16)
                    dve.load(flags, active[:, 0:NT])
                    for j in range(KF):
                        message(j, 0, 0)
                    one_hot(0, 0)
                    groups(dve, step)
                    dve.wait_ge(summed, 1)
                    nc.vector.tensor_copy(agg[:, 2:4, :], p_agg[1][:]).then_inc(agg_ok, 1)
                    nc.vector.tensor_copy(agg[:, 4, :], p_agg[2][:, 0, :]).then_inc(agg_ok, 1)

                @block.tensor
                def _(pe):
                    flags = [pe.alloc_register(f"pe_active{n}") for n in range(NT)]

                    def second_layer(g, par):
                        pe.wait_ge(hv_lo, g + 1)
                        for j in range(KF):
                            n = 0
                            for k in range(KF):
                                for wp, dp in PASSES:
                                    last = nc.tensor.matmul(p_v[j][:, 0:G], w2v_hl[wp][:, k, j * P:(j + 1) * P],
                                                            hvT_hl[par][dp][:, k, :], start=n == 0, stop=n == 5)
                                    n += 1
                            last.then_inc(v_psum, 1)

                    def step(i, b, first=False, last=False):
                        g = 4 * i + b
                        for j in range(KF):
                            pe.wait_ge(msgT_ok, KF * g + j + 1)
                            for t in range(T):
                                done = nc.tensor.transpose(p_msg[j][0:TP, t, :], msgT[:, j, t * TP:(t + 1) * TP],
                                                           ident[:])
                            done.then_inc(msg_psum, 1)
                        if not (last and b == 3):
                            second_layer(g + 1, (b + 1) % 2)
                        pe.load(flags, active[:, bass.ds(g * NT, NT)])
                        for n in range(NT):
                            with pe.If_ne(flags[n], 0):
                                pe.wait_ge(msg_lo, KF * g + KF)
                                for t in range(T):
                                    for part in range(2):
                                        nc.tensor.matmul(p_agg[n // 2][:, n % 2, :],
                                                         onehot[b % 2][:, t, n * TP:(n + 1) * TP],
                                                         msg[:, part, t, :], start=False, stop=False)

                    second_layer(0, 0)
                    pe.wait_ge(zero_ok, 2)
                    for bank in p_agg:
                        nc.tensor.matmul(bank[:], zeros_r[:, 0:TP], zeros_r[:], start=True, stop=False)
                    pe.wait_ge(active_in, 16)
                    groups(pe, step)
                    for bank in p_agg:
                        last = nc.tensor.matmul(bank[:], zeros_r[:, 0:TP], zeros_r[:], start=False, stop=True)
                    last.then_inc(summed, 1)

        msg_mem.close()

        with ExitStack() as s:
            NH = 2 * KH
            ND = 3
            acc = sb(s, "acc", [TP, NT, F])
            weight = sb(s, "weight", [TP, NT, NE])
            xnT = sb(s, "xnT", [P, KF, NPAD])
            xnT_hl = [sb(s, f"xnT_{n}", [P, KF, NPAD], F32R) for n in ("hi", "lo")]
            b1T = sb(s, "b1T", [P, NE * KH])
            ones = sb(s, "ones", [TP, TP])
            bn_rows = sb(s, "bn_rows", [TP, 2, F])
            gate_b = sb(s, "gate_b", [TP, 2, NE])
            dev = sb(s, "dev", [TP, NT, F])
            sq = sb(s, "sq", [TP, NT, F])
            rs = sb(s, "rs", [TP, F])
            wg_sb = sb(s, "wg_sb", [P, KF, NE])
            b1_sb = sb(s, "b1_sb", [NE * KH, P])
            b2_sb = sb(s, "b2_sb", [NE, F])
            expert_id = sb(s, "expert_id", [TP, NT, NE])
            rt = sb(s, "rt", [TP, 5, NT, NE])
            rs1 = sb(s, "rs1", [TP, 8, NT])
            wT = sb(s, "wT", [NE, NT, TP])
            b1e = [sb(s, f"b1e{b}", [P, KH]) for b in range(2)]
            hid = [sb(s, f"hid{b}", [P, 314]) for b in range(4)]
            hT_hl = [[sb(s, f"hT{b}_{n}", [P, KH, NPAD], F32R) for n in ("hi", "lo")] for b in range(2)]
            p_h = [ps(s, f"p_h{b}", [P, 512]) for b in range(4)]
            p_y01 = [ps(s, f"p_y{b}", [P, 512]) for b in range(2)]
            p_y = [bank[0:TP, 0:F] for bank in p_y01]
            p_a = ps(s, "p_a", [P, 512])
            p_b = ps(s, "p_b", [P, 512])
            p_sum, p_var = p_h[0][0:TP, 0:F], p_h[1][0:TP, 0:F]
            p_xnT = [bank[:, 0:KF * TP].rearrange("p (k n) -> p k n", k=KF)
                     for bank in (p_h[2], p_h[3], p_y01[0], p_y01[1], p_b)]
            b2_bank = (p_a, p_b, p_h[0])
            p_log = p_b[0:TP, 0:NT * NE].rearrange("p (t e) -> p t e", t=NT)
            (n_in, ids2_ok, ones_ok, chain2, pre_add, dev_ok, sum_psum, sq_ok, var_psum, std3_ok, std4_ok,
             x1_ok, xn_ok, xnT_psum, xnT_hi, xnT_lo, log_psum, log_ok, exp_ok, weight_ok, wT_psum, wT_ok,
             b1_psum, b1T_ok, b2_psum, b2_ok, pad_ok, h_psum, hid_ok, h_split, y_psum, y_added, out_in,
             bias_ok, xnT_ok, rs_ok, norm_ok) = sems(
                s, "n_in", "ids2_ok", "ones_ok", "chain2", "pre_add", "dev_ok", "sum_psum", "sq_ok", "var_psum",
                "std3_ok", "std4_ok", "x1_ok", "xn_ok", "xnT_psum", "xnT_hi_s", "xnT_lo_s", "log_psum",
                "log_ok", "exp_ok", "weight_ok", "wT_psum", "wT_ok", "b1_psum", "b1T_ok", "b2_psum",
                "b2_ok", "pad_ok", "h_psum", "hid_ok", "h_split", "y_psum", "y_added", "out_in", "bias_ok",
                "xnT_ok", "rs_ok", "norm_ok")
            logit, pick1, pick2, pen, rest = (rt[:, n] for n in range(5))
            top1, top2, diff, expd, id1, id2, w1st, w2nd = (rs1[:, n, :] for n in range(8))

            def over_experts(v):
                return v.rearrange("p (t a) -> p t a", a=1).broadcast_to((TP, NT, NE))

            def over_nodes(v):
                return v.rearrange("p (a e) -> p a e", a=1).broadcast_to((TP, NT, NE))

            with nc.Block(no_gpsimd_drain=True) as block:

                @block.sync
                def _(sp):
                    for n, v in enumerate((g_bn, beta_bn)):
                        sp.dma_start(bn_rows[:, n, :], spread(v, F)).then_inc(n_in, 16)
                    for n, v in enumerate((bg, bias)):
                        sp.dma_start(gate_b[:, n, :], spread(v, NE)).then_inc(n_in, 16)
                    sp.dma_start(wg_sb[:], Wg.rearrange("(k p) e -> p k e", p=P)).then_inc(n_in, 16)
                    sp.dma_start(b1_sb[:], b1.rearrange("e (m p) -> (e m) p", p=P)).then_inc(n_in, 16)
                    sp.dma_start(b2_sb[:], b2).then_inc(n_in, 16)
                    with sp.Fori(1, NE // 2) as i:
                        for b in range(2):
                            e = 2 * i + b
                            sp.wait_ge(w1e_lo, e - 1)
                            sp.dma_start(raw1[b][:], W1[e].rearrange("(k p) n -> p k n", p=P)).then_inc(
                                raw_in[b], 16)
                            sp.wait_ge(w2e_lo, e - 1)
                            sp.dma_start(raw2[b][:], W2[e].rearrange("(k p) n -> p k n", p=P)).then_inc(
                                raw_in[b], 16)
                    for t in range(NT):
                        sp.wait_ge(y_added, NT * NE - NT + t + 1)
                        for lo, up in ROWS:
                            sp.dma_start(out_v[lo:up, t, :], acc[lo:up, t, :]).then_inc(out_in, 16)
                    sp.wait_ge(out_in, 32 * NT)

                @block.gpsimd
                def _(pool):
                    pool.wait_ge(n_in, 16 * 7)
                    for t in range(NT):
                        nc.gpsimd.tensor_tensor(xln[:, t, :], xln[:, t, :], bn_rows[:, 1, :],
                                                ALU.add).then_inc(pre_add, 1)
                    nc.gpsimd.iota(expert_id[:], pattern=[[0, NT], [1, NE]], base=0, channel_multiplier=0,
                                   allow_small_or_imprecise_dtypes=True).then_inc(ids2_ok, 1)
                    pool.wait_ge(dev_ok, NT)
                    pool.wait_ge(sq_ok, NT)
                    pool.wait_ge(pre_add, NT)
                    pool.wait_ge(rs_ok, 1)
                    for t in range(ND, NT):
                        nc.gpsimd.tensor_tensor(dev[:, t, :], dev[:, t, :], rs[:], ALU.mult).then_inc(norm_ok, 1)
                    for t in range(ND, NT):
                        pool.wait_ge(norm_ok, t - ND + 1)
                        nc.gpsimd.tensor_tensor(dev[:, t, :], dev[:, t, :], xln[:, t, :], ALU.add).then_inc(norm_ok, 1)
                    for t in range(NT):
                        cols = slice(t * TP, (t + 1) * TP)
                        pool.wait_ge(xnT_lo, t + 1)
                        nc.gpsimd.tensor_tensor(xnT[:, :, cols], xnT_hl[0][:, :, cols], xnT_hl[1][:, :, cols],
                                                ALU.add).then_inc(xnT_ok, 1)

                @block.scalar
                def _(act):
                    nc.scalar.activation(warm[:], warm[:], ACT.Sqrt)
                    for t in range(NT):
                        act.wait_ge(dev_ok, t + 1)
                        nc.scalar.activation(sq[:, t, :], dev[:, t, :], ACT.Square).then_inc(sq_ok, 1)
                    act.wait_ge(chain2, 1)
                    nc.scalar.activation(rs[:], rs[:], ACT.Sqrt).then_inc(std3_ok, 1)
                    act.wait_ge(std4_ok, 1)
                    nc.scalar.activation(ln_std[:], ln_std[:], ACT.Sqrt).then_inc(std4_ok, 1)
                    act.wait_ge(pad_ok, 2)
                    nc.scalar.copy(xnT_hl[0][:, :, N:NPAD], xnT[:, :, N:NPAD]).then_inc(pad_ok, 1)
                    act.wait_ge(b1T_ok, 1)
                    for t in range(NT):
                        act.wait_ge(xnT_psum, t + 1)
                        nc.scalar.copy(xnT_hl[0][:, :, t * TP:(t + 1) * TP], p_xnT[t]).then_inc(xnT_hi, 1)
                    for b in range(2):
                        nc.scalar.copy(b1e[b][:], b1T[:, b * KH:(b + 1) * KH]).then_inc(bias_ok, 1)

                    def hidden(i, b, pieces=range(KH), first=False, start=False):
                        e = 2 * i + b
                        act.wait_ge(bias_ok, e + 1)
                        for m in pieces:
                            for q, (lo, up) in enumerate(HALF):
                                n = 2 * m + q
                                act.wait_ge(h_psum, NH * e + n + 1)
                                if not (start and n < 4):
                                    act.wait_ge(h_split, NH * e + n - 3)
                                if not first:
                                    act.wait_ge(y_psum, NT * (e - 1))
                                nc.scalar.activation(hT_hl[b][0][:, m, lo:up], p_h[n % 4][:, 0:up - lo], ACT.Relu,
                                                     bias=b1e[b][:, m:m + 1])
                                nc.scalar.activation(hid[n % 4][:, 0:up - lo], p_h[n % 4][:, 0:up - lo], ACT.Relu,
                                                     bias=b1e[b][:, m:m + 1]).then_inc(hid_ok, 1)

                    def split1(i, b):
                        e = 2 * i + b
                        act.wait_ge(raw_in[b], 32 * i + 32)
                        act.wait_ge(h_psum, NH * (e - 1))
                        nc.scalar.copy(w1e[b][0][:], raw1[b][:]).then_inc(w1e_hi, 1)
                        nc.scalar.copy(b1e[b][:], b1T[:, bass.ds(e * KH, KH)]).then_inc(bias_ok, 1)

                    def split2(i, b):
                        act.wait_ge(y_psum, NT * (2 * i + b - 1))
                        nc.scalar.copy(w2e[b][0][:], raw2[b][:]).then_inc(w2e_hi, 1)

                    hidden(0, 0, first=True, start=True)
                    nc.scalar.activation(warm[:], warm[:], ACT.Exp)
                    hidden(0, 1, pieces=range(2), first=True)
                    act.wait_ge(log_ok, 1)
                    nc.scalar.activation(expd, diff, ACT.Exp).then_inc(exp_ok, 1)
                    hidden(0, 1, pieces=range(2, KH), first=True)
                    split1(1, 0)
                    with act.Fori(1, NE // 2 - 1) as i:
                        hidden(i, 0)
                        split1(i, 1)
                        split2(i, 0)
                        hidden(i, 1)
                        split1(i + 1, 0)
                        split2(i, 1)
                    hidden(NE // 2 - 1, 0)
                    split1(NE // 2 - 1, 1)
                    split2(NE // 2 - 1, 0)
                    hidden(NE // 2 - 1, 1)
                    split2(NE // 2 - 1, 1)

                @block.vector
                def _(dve):
                    done = [0]

                    def then(ins):
                        done[0] += 1
                        ins.then_inc(chain2, 1)
                        dve.wait_ge(chain2, done[0])

                    nc.vector.memset(ones[:], 1.0).then_inc(ones_ok, 1)
                    nc.vector.memset(xnT[:, :, N:NPAD], 0.0).then_inc(pad_ok, 1)
                    dve.wait_ge(pad_ok, 1)
                    nc.vector.tensor_copy(xnT_hl[1][:, :, N:NPAD], xnT[:, :, N:NPAD]).then_inc(pad_ok, 1)
                    dve.wait_ge(sum_psum, 1)
                    for t in range(NT):
                        nc.vector.scalar_tensor_tensor(out=dev[:, t, :], in0=p_sum, scalar=-1.0 / N,
                                                       in1=agg[:, t, :], op0=ALU.mult, op1=ALU.add).then_inc(dev_ok, 1)
                    dve.wait_ge(var_psum, 1)
                    then(nc.vector.tensor_scalar(rs[:], p_var, 1.0 / N, EPS, ALU.mult, ALU.add))
                    dve.wait_ge(std3_ok, 1)
                    then(nc.vector.reciprocal(rs[:], rs[:]))
                    dve.wait_ge(n_in, 16 * 7)
                    then(nc.vector.tensor_tensor(rs[:], rs[:], bn_rows[:, 0, :], ALU.mult))
                    dve.sem_inc(rs_ok, 1)
                    base = done[0]
                    dve.wait_ge(dev_ok, NT)
                    dve.wait_ge(sq_ok, NT)
                    for t in range(ND):
                        nc.vector.tensor_tensor(dev[:, t, :], dev[:, t, :], rs[:], ALU.mult).then_inc(chain2, 1)
                    for t in range(ND):
                        dve.wait_ge(chain2, base + t + 1)
                        dve.wait_ge(pre_add, t + 1)
                        nc.vector.tensor_tensor(dev[:, t, :], dev[:, t, :], xln[:, t, :], ALU.add).then_inc(chain2, 1)
                    for t in range(NT):
                        if t < ND:
                            dve.wait_ge(chain2, base + ND + t + 1)
                        else:
                            dve.wait_ge(norm_ok, 2 * (NT - ND) - NT + t + 1)
                        nc.vector.scalar_tensor_tensor(out=x_sb[:, t, :], in0=dev[:, t, :], scalar=0.0,
                                                       in1=x_sb[:, t, :], op0=ALU.max, op1=ALU.add).then_inc(x1_ok, 1)
                    for t in range(NT):
                        dve.wait_ge(x1_ok, t + 1)
                        nc.vector.bn_stats(ln_stats[:, t, :], x_sb[:, t, :]).then_inc(chain2, 1)
                    for t in range(NT):
                        dve.wait_ge(chain2, base + 2 * ND + t + 1)
                        nc.vector.bn_aggr(ln_mv[:, t, :], ln_stats[:, t, :]).then_inc(chain2, 1)
                    dve.wait_ge(chain2, base + 2 * ND + 2 * NT)
                    done[0] = base + 2 * ND + 2 * NT
                    nc.vector.tensor_scalar(ln_std[:], ln_mv[:, :, 1], EPS, None, ALU.add).then_inc(std4_ok, 1)
                    dve.wait_ge(std4_ok, 2)
                    then(nc.vector.reciprocal(ln_std[:], ln_std[:]))
                    for t in range(NT):
                        nc.vector.tensor_scalar(xln[:, t, :], x_sb[:, t, :], ln_mv[:, t, 0:1], ln_std[:, t:t + 1],
                                                ALU.subtract, ALU.mult).then_inc(xn_ok, 1)
                    dve.wait_ge(b1_psum, 1)
                    nc.vector.tensor_copy(b1T[:], p_a[:, 0:NE * KH]).then_inc(b1T_ok, 1)
                    for t in range(NT):
                        dve.wait_ge(xnT_hi, t + 1)
                        nc.vector.tensor_tensor(xnT_hl[1][:, :, t * TP:(t + 1) * TP], p_xnT[t],
                                                xnT_hl[0][:, :, t * TP:(t + 1) * TP], ALU.subtract).then_inc(xnT_lo, 1)

                    def hidden_lo(i, b, pieces=range(KH)):
                        for m in pieces:
                            for q, (lo, up) in enumerate(HALF):
                                n = 2 * m + q
                                dve.wait_ge(hid_ok, NH * (2 * i + b) + n + 1)
                                nc.vector.tensor_tensor(hT_hl[b][1][:, m, lo:up], hid[n % 4][:, 0:up - lo],
                                                        hT_hl[b][0][:, m, lo:up], ALU.subtract).then_inc(h_split, 1)

                    def split1(i, b):
                        dve.wait_ge(w1e_hi, 2 * i + b + 1)
                        nc.vector.tensor_tensor(w1e[b][1][:], raw1[b][:], w1e[b][0][:],
                                                ALU.subtract).then_inc(w1e_lo, 1)

                    def split2(i, b):
                        dve.wait_ge(w2e_hi, 2 * i + b + 1)
                        nc.vector.tensor_tensor(w2e[b][1][:], raw2[b][:], w2e[b][0][:],
                                                ALU.subtract).then_inc(w2e_lo, 1)

                    def add(i, b, tiles=range(NT), first=False):
                        e = 2 * i + b
                        for t in tiles:
                            dve.wait_ge(y_psum, NT * e + t + 1)
                            if not first:
                                dve.wait_ge(y_added, NT * e - NT + t + 1)
                            nc.vector.scalar_tensor_tensor(out=acc[:, t, :], in0=p_y[(b + t) % 2],
                                                           scalar=weight[:, t, bass.ds(e, 1)],
                                                           in1=x_sb[:, t, :] if first else acc[:, t, :],
                                                           op0=ALU.mult, op1=ALU.add).then_inc(y_added, 1)

                    def pick(table, top, number, chosen):
                        then(nc.vector.tensor_reduce(top, table, AX_X, ALU.max))
                        then(nc.vector.tensor_tensor(pen, table, over_experts(top), ALU.is_lt))
                        then(nc.vector.scalar_tensor_tensor(out=pen, in0=pen, scalar=float(NE), in1=expert_id[:],
                                                            op0=ALU.mult, op1=ALU.add))
                        then(nc.vector.tensor_reduce(number, pen, AX_X, ALU.min))
                        then(nc.vector.tensor_tensor(chosen, expert_id[:], over_experts(number), ALU.is_equal))

                    early, late = range(2), range(2, NT)
                    hidden_lo(0, 0)
                    dve.wait_ge(log_psum, 1)
                    dve.wait_ge(ids2_ok, 1)
                    then(nc.vector.tensor_tensor(logit, p_log, over_nodes(gate_b[:, 0, :]), ALU.add))
                    then(nc.vector.tensor_tensor(logit, logit, over_nodes(gate_b[:, 1, :]), ALU.add))
                    pick(logit, top1, id1, pick1)
                    then(nc.vector.scalar_tensor_tensor(out=rest, in0=pick1, scalar=-3.0e38, in1=logit,
                                                        op0=ALU.mult, op1=ALU.add))
                    pick(rest, top2, id2, pick2)
                    nc.vector.tensor_tensor(diff, top2, top1, ALU.subtract).then_inc(log_ok, 1)
                    hidden_lo(0, 1, range(KH - 1))
                    dve.wait_ge(exp_ok, 1)
                    then(nc.vector.tensor_scalar(w1st, expd, 1.0, None, ALU.add))
                    then(nc.vector.reciprocal(w1st, w1st))
                    then(nc.vector.tensor_tensor(w2nd, expd, w1st, ALU.mult))
                    then(nc.vector.tensor_tensor(pick1, pick1, over_experts(w1st), ALU.mult))
                    then(nc.vector.tensor_tensor(pick2, pick2, over_experts(w2nd), ALU.mult))
                    nc.vector.tensor_tensor(weight[:], pick1, pick2, ALU.add).then_inc(weight_ok, 1)
                    hidden_lo(0, 1, range(KH - 1, KH))
                    dve.wait_ge(weight_ok, 1)
                    add(0, 0, early, first=True)
                    split1(1, 0)
                    add(0, 0, late, first=True)
                    dve.wait_ge(wT_psum, 1)
                    nc.vector.tensor_copy(wT[:, 0:4, :], p_a[0:NE, 0:4 * TP].rearrange(
                        "e (t n) -> e t n", t=4)).then_inc(wT_ok, 1)
                    nc.vector.tensor_copy(wT[:, 4, :], p_b[0:NE, 0:TP]).then_inc(wT_ok, 1)
                    with dve.Fori(1, NE // 2 - 1) as i:
                        hidden_lo(i, 0)
                        add(i - 1, 1, early)
                        split1(i, 1)
                        add(i - 1, 1, late)
                        split2(i, 0)
                        hidden_lo(i, 1)
                        add(i, 0, early)
                        split1(i + 1, 0)
                        add(i, 0, late)
                        split2(i, 1)
                    hidden_lo(NE // 2 - 1, 0)
                    add(NE // 2 - 2, 1, early)
                    split1(NE // 2 - 1, 1)
                    add(NE // 2 - 2, 1, late)
                    split2(NE // 2 - 1, 0)
                    hidden_lo(NE // 2 - 1, 1)
                    add(NE // 2 - 1, 0, early)
                    split2(NE // 2 - 1, 1)
                    add(NE // 2 - 1, 0, late)
                    before = NT * (NE - 1)
                    for t in range(NT):
                        dve.wait_ge(b2_psum, 1 + (t + 1) // 5)
                        dve.wait_ge(y_added, before)
                        bank = b2_bank[t // 2][0:TP, (t % 2) * F:(t % 2 + 1) * F]
                        nc.vector.tensor_tensor(acc[:, t, :], bank, acc[:, t, :], ALU.add).then_inc(b2_ok, 1)
                    dve.wait_ge(b2_ok, NT)
                    add(NE // 2 - 1, 1)

                @block.tensor
                def _(pe):
                    pe.wait_ge(ones_ok, 1)
                    for t in range(NT):
                        last = nc.tensor.matmul(p_sum, ones[:], agg[:, t, :], start=t == 0, stop=t == NT - 1)
                    last.then_inc(sum_psum, 1)
                    pe.wait_ge(n_in, 16 * 7)
                    nc.tensor.transpose(p_a[:, 0:NE * KH], b1_sb[:], ident[0:NE * KH, 0:NE * KH]).then_inc(
                        b1_psum, 1)
                    for t in range(NT):
                        pe.wait_ge(sq_ok, t + 1)
                        last = nc.tensor.matmul(p_var, ones[:], sq[:, t, :], start=t == 0, stop=t == NT - 1)
                    last.then_inc(var_psum, 1)
                    for t in range(NT):
                        pe.wait_ge(xn_ok, t + 1)
                        for k in range(KF):
                            last = nc.tensor.transpose(p_xnT[t][:, k, :], xln[:, t, k * P:(k + 1) * P],
                                                       ident[0:TP, 0:TP])
                        last.then_inc(xnT_psum, 1)
                    def first_product(i, b, first=False):
                        e = 2 * i + b
                        pe.wait_ge(w1e_lo, e + 1)
                        for m in range(KH):
                            for h, (lo, up) in enumerate(HALF):
                                n = 2 * m + h
                                if not (first and n < 4):
                                    pe.wait_ge(hid_ok, NH * e + n - 3)
                                q = 0
                                for k in range(KF):
                                    for wp, dp in PASSES:
                                        last = nc.tensor.matmul(p_h[n % 4][:, 0:up - lo],
                                                                w1e[b][wp][:, k, m * P:(m + 1) * P],
                                                                xnT_hl[dp][:, k, lo:up], start=q == 0, stop=q == 5)
                                        q += 1
                                last.then_inc(h_psum, 1)

                    def second_product(i, b, first=False):
                        e = 2 * i + b
                        pe.wait_ge(w2e_lo, e + 1)
                        pe.wait_ge(h_split, NH * e + NH)
                        for t in range(NT):
                            if not (first and t < 2):
                                pe.wait_ge(y_added, NT * e + t - 1)
                            q = 0
                            for k in range(KH):
                                for wp, dp in PASSES:
                                    last = nc.tensor.matmul(p_y[(b + t) % 2],
                                                            hT_hl[b][dp][:, k, t * TP:(t + 1) * TP],
                                                            w2e[b][wp][:, k, :], start=q == 0,
                                                            stop=q == 3 * KH - 1)
                                    q += 1
                            last.then_inc(y_psum, 1)

                    pe.wait_ge(xnT_lo, NT)
                    pe.wait_ge(pad_ok, 3)
                    first_product(0, 0, first=True)
                    pe.wait_ge(xnT_ok, NT)
                    for t in range(NT):
                        for k in range(KF):
                            last = nc.tensor.matmul(p_log[:, t, :], xnT[:, k, t * TP:(t + 1) * TP], wg_sb[:, k, :],
                                                    start=k == 0, stop=k == KF - 1)
                    last.then_inc(log_psum, 1)
                    first_product(0, 1)
                    second_product(0, 0, first=True)
                    pe.wait_ge(weight_ok, 1)
                    pe.wait_ge(b1T_ok, 1)
                    for t in range(NT):
                        to = p_a[0:NE, t * TP:(t + 1) * TP] if t < 4 else p_b[0:NE, 0:TP]
                        last = nc.tensor.transpose(to, weight[:, t, :], ident[0:TP, 0:TP])
                    last.then_inc(wT_psum, 1)
                    with pe.Fori(1, NE // 2) as i:
                        first_product(i, 0)
                        second_product(i - 1, 1)
                        first_product(i, 1)
                        second_product(i, 0)
                    pe.wait_ge(wT_ok, 2)
                    for t in range(NT):
                        if t == 4:
                            pe.wait_ge(h_split, NH * NE)
                        bank = b2_bank[t // 2][0:TP, (t % 2) * F:(t % 2 + 1) * F]
                        last = nc.tensor.matmul(bank, wT[:, t, :], b2_sb[:], start=True, stop=True)
                        if t >= 3:
                            last.then_inc(b2_psum, 1)
                    second_product(NE // 2 - 1, 1)


_INS = ["x", "src", "dst", "edge_attr_256", "L0_gnn_W1f", "L0_gnn_b1f", "L0_gnn_W2f", "L0_gnn_b2f", "L0_gnn_W1m",
        "L0_gnn_b1m", "L0_gnn_W2m", "L0_gnn_b2m", "L0_gnn_g_int", "L0_gnn_beta_int", "L0_gnn_g_bn",
        "L0_gnn_beta_bn", "L0_ffn_Wg", "L0_ffn_bg", "L0_ffn_bias", "L0_ffn_W1", "L0_ffn_b1", "L0_ffn_W2",
        "L0_ffn_b2"]


def kernel(**inputs):
    import numpy as _np
    import concourse.bacc as _bacc
    from concourse import mybir as _mybir
    from concourse.bass_utils import run_bass_kernel_spmd as _run

    nc = _bacc.Bacc("TRN2", target_bir_lowering=False, num_devices=1)
    arrays, args = {}, []
    for name in _INS:
        a = _np.ascontiguousarray(inputs[name])
        arrays[f"in_{name}_dram"] = a
        args.append(nc.dram_tensor(f"in_{name}_dram", a.shape, _mybir.dt.from_np(a.dtype), kind="ExternalInput").ap())
    out = nc.dram_tensor("out_0_dram", inputs["x"].shape, _mybir.dt.float32, kind="ExternalOutput").ap()
    gnn_moe(nc, *args, out)
    r = _run(nc, [arrays], core_ids=[0])
    return r.results[0]["out_0_dram"]
```
